# Optimizing a Trainium2 kernel written in Bass

```python
import numpy as np
import jax
import jax.numpy as jnp

def _softmax(x, axis=-1):
    return jax.nn.softmax(x, axis=axis)

def _gelu(x):
    return jax.nn.gelu(x, approximate=True)

def _silu(x):
    return jax.nn.silu(x)

def _sigmoid(x):
    return jax.nn.sigmoid(x)

def _layernorm(x, axis=-1, eps=1e-05):
    m = jnp.mean(x, axis=axis, keepdims=True)
    v = jnp.var(x, axis=axis, keepdims=True)
    return (x - m) / jnp.sqrt(v + eps)

def _scatter_add(tgt, idx, src, axis=0):
    return tgt.at[idx].add(src)

def _segment_sum(src, seg, n):
    return jax.ops.segment_sum(src, seg, n)
kernel_name = 'mk_flamingo_gated_d4_seqx_r8_3ce2c0'

def setup_inputs(seed: int=0):
    np.random.seed(seed)
    _w = jnp.asarray

    def _rec_inputs():
        import jax
        import jax.numpy as jnp
        _rk = jax.random.key(seed)
        x = -0.0002928 + 1 * jax.random.normal(jax.random.fold_in(_rk, 1), (16, 128, 256), jnp.float32)
        _lenS = 128 - jax.random.randint(jax.random.fold_in(_rk, 7), (16,), 0, max(1, 128 // 4) + 1, jnp.int32)
        _lenS2 = 128 - jax.random.randint(jax.random.fold_in(_rk, 8), (16,), 0, max(1, 128 // 4) + 1, jnp.int32)
        fside_S2_0 = -0.00337071 + 1.01897 * jax.random.normal(jax.random.fold_in(_rk, 11), (128,), jnp.float32)
        _ctx_2048P = jax.random.normal(jax.random.fold_in(_rk, 12), (16, 16, 256), jnp.float32)
        _ctx_2048c = jax.random.dirichlet(jax.random.fold_in(_rk, 512), 0.3 * jnp.ones((16,), jnp.float32), (16, 128))
        _ctx_2048t = jnp.einsum('bsk,bkd->bsd', _ctx_2048c, _ctx_2048P)
        _ctx_2048t = _ctx_2048t * jax.lax.rsqrt(jnp.mean(jnp.square(_ctx_2048t)) + 1e-12) * 0.953939
        ctx_2048 = 0.000675642 + 1.00031 * (_ctx_2048t + 0.3 * jax.random.normal(jax.random.fold_in(_rk, 612), (16, 128, 256), jnp.float32))
        _validS = jnp.arange(128)[None, :] < _lenS[:, None]
        _validS2 = jnp.arange(128)[None, :] < _lenS2[:, None]
        _causal = jnp.tril(jnp.ones((128, 128), dtype=bool))
        mask_BxS2_ik0 = jnp.where(jnp.broadcast_to(_validS2[:, :], (16, 128)), 0, 1).astype(jnp.int32)
        mask_BxSxS2_ff0 = jnp.where(jnp.ones((16, 128, 128), dtype=bool), 0.0, -1000000000.0).astype(jnp.float32)
        _g = jax.random.normal(jax.random.fold_in(_rk, 9001), (2, 4), jnp.float32)
        _g = jnp.sign(_g) * jnp.maximum(jnp.abs(_g), 1.0) + (_g == 0) * 1.0
        g_xattn = _g[0]
        g_ffn = _g[1]
        return (x, fside_S2_0, ctx_2048, mask_BxS2_ik0, mask_BxSxS2_ff0, g_xattn, g_ffn)
    x, fside_S2_0, ctx_2048, mask_BxS2_ik0, mask_BxSxS2_ff0, g_xattn, g_ffn = _rec_inputs()

    def _L0_xattn_setup():
        import jax, jax.numpy as jnp
        import numpy as np
        key = jax.random.key(seed)
        ks = jax.random.split(key, 5)
        B, D, L, NH = (2, 128, 256, 8)
        H = D // NH
        return {'v': jax.random.normal(ks[0], (B, D, L), jnp.float32), 'k': jax.random.normal(ks[1], (H, L), jnp.float32) * 0.1, 'bias': jax.random.normal(ks[2], (D,), jnp.float32), 'x1': jax.random.normal(ks[3], (B, D, L), jnp.float32), 'x2': jax.random.normal(ks[4], (B, D, L), jnp.float32), 'num_heads': NH}
    _L0_xattn_all = _L0_xattn_setup()
    _L0_xattn_in = {k: v for k, v in _L0_xattn_all.items() if k in ('k',)}
    del _L0_xattn_all

    def _L0_ffn_setup():
        import jax, jax.numpy as jnp
        import numpy as np
        HIDDEN = 256
        INTER = 96
        N_EXPERTS = 32
        TOP_K = 8
        key = jax.random.key(seed)
        k = jax.random.split(key, 5)
        s = 1.0 / np.sqrt(HIDDEN)
        return {'hidden_states': jax.random.normal(k[0], (1, 128, HIDDEN), jnp.float32), 'gate_w': jax.random.normal(k[1], (HIDDEN, N_EXPERTS), jnp.float32) * s, 'w_gate': jax.random.normal(k[2], (N_EXPERTS, HIDDEN, INTER), jnp.float32) * s, 'w_up': jax.random.normal(k[3], (N_EXPERTS, HIDDEN, INTER), jnp.float32) * s, 'w_down': jax.random.normal(k[4], (N_EXPERTS, INTER, HIDDEN), jnp.float32) * (1.0 / np.sqrt(INTER))}
    _L0_ffn_all = _L0_ffn_setup()
    _L0_ffn_in = {k: v for k, v in _L0_ffn_all.items() if k in ('gate_w', 'w_gate', 'w_up', 'w_down')}
    del _L0_ffn_all

    def _L1_xattn_setup():
        import jax, jax.numpy as jnp
        import numpy as np
        import math
        H = 256
        NH = 16
        HD = H // NH
        EPS_LN = 1e-05
        RES_SCALE_MAX = 0.3

        def _nan_clean(x, lim=10000.0):
            return jnp.nan_to_num(x, nan=0.0, posinf=lim, neginf=-lim)
        key = jax.random.key(seed)
        ks = jax.random.split(key, 12)
        B, S, T = (4, 256, 32)
        std = 1.0 / math.sqrt(H)
        return {'hidden_states': jax.random.normal(ks[0], (B, S, H), jnp.float32), 'audio_tokens': jax.random.normal(ks[1], (B, T, H), jnp.float32), 'attention_mask': jax.random.randint(ks[2], (B, T), 0, 2, jnp.int32), 'Wq': jax.random.normal(ks[3], (H, H), jnp.float32) * std, 'bq': jnp.zeros((H,), jnp.float32), 'Wk': jax.random.normal(ks[4], (H, H), jnp.float32) * std, 'bk': jnp.zeros((H,), jnp.float32), 'Wv': jax.random.normal(ks[5], (H, H), jnp.float32) * std, 'bv': jnp.zeros((H,), jnp.float32), 'Wo': jax.random.normal(ks[6], (H, H), jnp.float32) * std, 'bo': jnp.zeros((H,), jnp.float32), 'ln_gamma': jnp.ones((H,), jnp.float32), 'ln_beta': jnp.zeros((H,), jnp.float32), 'residual_scale': jnp.float32(0.05)}
    _L1_xattn_all = _L1_xattn_setup()
    _L1_xattn_in = {k: v for k, v in _L1_xattn_all.items() if k in ('Wq', 'bq', 'Wk', 'bk', 'Wv', 'bv', 'Wo', 'bo', 'ln_gamma', 'ln_beta', 'residual_scale')}
    del _L1_xattn_all

    def _L1_ffn_setup():
        import jax, jax.numpy as jnp
        import numpy as np
        import math
        N_EMBD = 256
        N_HEAD = 16
        HEAD_DIM = N_EMBD // N_HEAD
        B, T = (2, 256)
        key = jax.random.key(seed)
        k1, k2, k3 = jax.random.split(key, 3)
        x = jax.random.normal(k1, (B, T, N_EMBD), dtype=jnp.float32)
        W_gate = jax.random.normal(k2, (N_HEAD, N_EMBD), dtype=jnp.float32) * 0.02
        W_qkv = jax.random.normal(k3, (3 * N_EMBD, N_EMBD), dtype=jnp.float32) * 0.02
        return {'x': x, 'W_gate': W_gate, 'W_qkv': W_qkv}
    _L1_ffn_all = _L1_ffn_setup()
    _L1_ffn_in = {k: v for k, v in _L1_ffn_all.items() if k in ('W_gate', 'W_qkv')}
    del _L1_ffn_all

    def _L2_xattn_setup():
        import jax, jax.numpy as jnp
        import numpy as np
        HIDDEN = 256
        NUM_HEADS = 16
        NUM_KV_HEADS = 4
        HEAD_DIM = 128
        ROPE_THETA = 10000.0
        EPS = 1e-06

        def rms_norm(x, w, eps=EPS):
            var = jnp.mean(jnp.square(x), axis=-1, keepdims=True)
            return x * jax.lax.rsqrt(var + eps) * w

        def rope_cache(L, head_dim, theta, dtype):
            inv_freq = 1.0 / theta ** (jnp.arange(0, head_dim, 2, dtype=jnp.float32) / head_dim)
            t = jnp.arange(L, dtype=jnp.float32)
            freqs = jnp.outer(t, inv_freq)
            emb = jnp.concatenate([freqs, freqs], -1)
            cos = jnp.cos(emb).astype(dtype)[None, :, None, :]
            sin = jnp.sin(emb).astype(dtype)[None, :, None, :]
            return (cos, sin)

        def rotate_half(x):
            x1, x2 = jnp.split(x, 2, axis=-1)
            return jnp.concatenate([-x2, x1], axis=-1)
        key = jax.random.key(seed)
        ks = jax.random.split(key, 10)
        B, L, T = (2, 256, 64)
        q_out = NUM_HEADS * HEAD_DIM
        kv_out = NUM_KV_HEADS * HEAD_DIM
        s = lambda fan_in: 1.0 / np.sqrt(fan_in)
        return {'x': jax.random.normal(ks[0], (B, L, HIDDEN), jnp.float32), 'h_ctx_kv': jax.random.normal(ks[1], (B, T, HIDDEN), jnp.float32), 'wq': jax.random.normal(ks[2], (HIDDEN, q_out), jnp.float32) * s(HIDDEN), 'wk': jax.random.normal(ks[3], (HIDDEN, kv_out), jnp.float32) * s(HIDDEN), 'wv': jax.random.normal(ks[4], (HIDDEN, kv_out), jnp.float32) * s(HIDDEN), 'wo': jax.random.normal(ks[5], (q_out, HIDDEN), jnp.float32) * s(q_out), 'wk_ctx': jax.random.normal(ks[6], (HIDDEN, kv_out), jnp.float32) * s(HIDDEN), 'wv_ctx': jax.random.normal(ks[7], (HIDDEN, kv_out), jnp.float32) * s(HIDDEN), 'q_norm_w': jnp.ones((HEAD_DIM,), jnp.float32), 'k_norm_w': jnp.ones((HEAD_DIM,), jnp.float32)}
    _L2_xattn_all = _L2_xattn_setup()
    _L2_xattn_in = {k: v for k, v in _L2_xattn_all.items() if k in ('wq', 'wk', 'wv', 'wo', 'wk_ctx', 'wv_ctx', 'q_norm_w', 'k_norm_w')}
    del _L2_xattn_all

    def _L2_ffn_setup():
        import jax, jax.numpy as jnp
        import numpy as np
        D_MODEL = 256
        HIDDEN = 4 * D_MODEL
        B, S = (2, 512)

        def bit_linear(x, w, b):
            gamma_x = jnp.clip(jnp.max(jnp.abs(x), axis=-1, keepdims=True), 1e-05, None)
            scale_x = 127.0 / gamma_x
            x_dq = jnp.clip(jnp.round(x * scale_x), -128.0, 127.0) / scale_x
            x_ste = x + jax.lax.stop_gradient(x_dq - x)
            gamma_w = jnp.clip(jnp.mean(jnp.abs(w)), 1e-05, None)
            w_dq = jnp.clip(jnp.round(w / gamma_w), -1.0, 1.0) * gamma_w
            w_ste = w + jax.lax.stop_gradient(w_dq - w)
            return jnp.einsum('bsd,hd->bsh', x_ste, w_ste) + b
        key = jax.random.key(seed)
        ks = jax.random.split(key, 7)
        std = 0.02
        return {'x': jax.random.normal(ks[0], (B, S, D_MODEL), dtype=jnp.float32), 'gate_w': jax.random.normal(ks[1], (HIDDEN, D_MODEL), dtype=jnp.float32) * std, 'gate_b': jnp.zeros((HIDDEN,), dtype=jnp.float32), 'val_w': jax.random.normal(ks[2], (HIDDEN, D_MODEL), dtype=jnp.float32) * std, 'val_b': jnp.zeros((HIDDEN,), dtype=jnp.float32), 'out_w': jax.random.normal(ks[3], (D_MODEL, HIDDEN), dtype=jnp.float32) * std, 'out_b': jnp.zeros((D_MODEL,), dtype=jnp.float32)}
    _L2_ffn_all = _L2_ffn_setup()
    _L2_ffn_in = {k: v for k, v in _L2_ffn_all.items() if k in ('gate_w', 'gate_b', 'val_w', 'val_b', 'out_w', 'out_b')}
    del _L2_ffn_all

    def _L3_xattn_setup():
        import jax, jax.numpy as jnp
        import numpy as np
        NUM_HEADS = 16
        EPS = 1e-08

        def _dyn_quant(x):
            s = jnp.maximum(jnp.max(jnp.abs(x), axis=-1, keepdims=True) / 127.0, EPS)
            q = jnp.clip(jnp.round(x / s), -127.0, 127.0)
            return (q, s)

        def _quant_weight(w):
            s = jnp.maximum(jnp.max(jnp.abs(w), axis=1, keepdims=True) / 127.0, EPS)
            q = jnp.clip(jnp.round(w / s), -127.0, 127.0)
            return (q, s)

        def _w8a8_linear(x, w, b):
            qx, sx = _dyn_quant(x)
            qw, sw = _quant_weight(w)
            y = jnp.einsum('bnc,oc->bno', qx, qw) * (sx * sw[:, 0])
            return y + b
        key = jax.random.key(seed)
        ks = jax.random.split(key, 9)
        B, N, L, C = (2, 512, 64, 256)
        sc = 0.02
        return {'x': jax.random.normal(ks[0], (B, N, C), jnp.float32), 'cond': jax.random.normal(ks[1], (B, L, C), jnp.float32), 'mask': jnp.zeros((B, N, L), jnp.float32), 'wq': jax.random.normal(ks[2], (C, C), jnp.float32) * sc, 'bq': jnp.zeros((C,), jnp.float32), 'wk': jax.random.normal(ks[3], (C, C), jnp.float32) * sc, 'bk': jnp.zeros((C,), jnp.float32), 'wv': jax.random.normal(ks[4], (C, C), jnp.float32) * sc, 'bv': jnp.zeros((C,), jnp.float32), 'wo': jax.random.normal(ks[5], (C, C), jnp.float32) * sc, 'bo': jnp.zeros((C,), jnp.float32)}
    _L3_xattn_all = _L3_xattn_setup()
    _L3_xattn_in = {k: v for k, v in _L3_xattn_all.items() if k in ('wq', 'bq', 'wk', 'bk', 'wv', 'bv', 'wo', 'bo')}
    del _L3_xattn_all

    def _L3_ffn_setup():
        import jax, jax.numpy as jnp
        import numpy as np
        B, S, D = (2, 256, 256)
        E = 8
        TOPK = 2
        H_SHARED = 1024
        H_ROUTED = 128
        STD = 0.02
        key = jax.random.key(seed)
        ks = jax.random.split(key, 7)
        return {'x': jax.random.normal(ks[0], (B, S, D), jnp.float32), 'w12': jax.random.normal(ks[1], (E, 2 * H_ROUTED, D), jnp.float32) * STD, 'w3': jax.random.normal(ks[2], (E, D, H_ROUTED), jnp.float32) * STD, 'router_w': jax.random.normal(ks[3], (E, D), jnp.float32) * STD, 'expert_bias': jnp.zeros((E,), jnp.float32), 'sw1': jax.random.normal(ks[4], (H_SHARED, D), jnp.float32) * STD, 'sw2': jax.random.normal(ks[5], (H_SHARED, D), jnp.float32) * STD, 'sw3': jax.random.normal(ks[6], (D, H_SHARED), jnp.float32) * STD}
    _L3_ffn_all = _L3_ffn_setup()
    _L3_ffn_in = {k: v for k, v in _L3_ffn_all.items() if k in ('w12', 'w3', 'router_w', 'expert_bias', 'sw1', 'sw2', 'sw3')}
    del _L3_ffn_all
    return {'x': x, 'fside_S2_0': fside_S2_0, 'ctx_2048': ctx_2048, 'mask_BxS2_ik0': mask_BxS2_ik0, 'mask_BxSxS2_ff0': mask_BxSxS2_ff0, 'g_xattn': g_xattn, 'g_ffn': g_ffn, 'L0_xattn_k': _L0_xattn_in['k'], 'L0_ffn_gate_w': _L0_ffn_in['gate_w'], 'L0_ffn_w_gate': _L0_ffn_in['w_gate'], 'L0_ffn_w_up': _L0_ffn_in['w_up'], 'L0_ffn_w_down': _L0_ffn_in['w_down'], 'L1_xattn_Wq': _L1_xattn_in['Wq'], 'L1_xattn_bq': _L1_xattn_in['bq'], 'L1_xattn_Wk': _L1_xattn_in['Wk'], 'L1_xattn_bk': _L1_xattn_in['bk'], 'L1_xattn_Wv': _L1_xattn_in['Wv'], 'L1_xattn_bv': _L1_xattn_in['bv'], 'L1_xattn_Wo': _L1_xattn_in['Wo'], 'L1_xattn_bo': _L1_xattn_in['bo'], 'L1_xattn_ln_gamma': _L1_xattn_in['ln_gamma'], 'L1_xattn_ln_beta': _L1_xattn_in['ln_beta'], 'L1_xattn_residual_scale': _L1_xattn_in['residual_scale'], 'L1_ffn_W_gate': _L1_ffn_in['W_gate'], 'L1_ffn_W_qkv': _L1_ffn_in['W_qkv'], 'L2_xattn_wq': _L2_xattn_in['wq'], 'L2_xattn_wk': _L2_xattn_in['wk'], 'L2_xattn_wv': _L2_xattn_in['wv'], 'L2_xattn_wo': _L2_xattn_in['wo'], 'L2_xattn_wk_ctx': _L2_xattn_in['wk_ctx'], 'L2_xattn_wv_ctx': _L2_xattn_in['wv_ctx'], 'L2_xattn_q_norm_w': _L2_xattn_in['q_norm_w'], 'L2_xattn_k_norm_w': _L2_xattn_in['k_norm_w'], 'L2_ffn_gate_w': _L2_ffn_in['gate_w'], 'L2_ffn_gate_b': _L2_ffn_in['gate_b'], 'L2_ffn_val_w': _L2_ffn_in['val_w'], 'L2_ffn_val_b': _L2_ffn_in['val_b'], 'L2_ffn_out_w': _L2_ffn_in['out_w'], 'L2_ffn_out_b': _L2_ffn_in['out_b'], 'L3_xattn_wq': _L3_xattn_in['wq'], 'L3_xattn_bq': _L3_xattn_in['bq'], 'L3_xattn_wk': _L3_xattn_in['wk'], 'L3_xattn_bk': _L3_xattn_in['bk'], 'L3_xattn_wv': _L3_xattn_in['wv'], 'L3_xattn_bv': _L3_xattn_in['bv'], 'L3_xattn_wo': _L3_xattn_in['wo'], 'L3_xattn_bo': _L3_xattn_in['bo'], 'L3_ffn_w12': _L3_ffn_in['w12'], 'L3_ffn_w3': _L3_ffn_in['w3'], 'L3_ffn_router_w': _L3_ffn_in['router_w'], 'L3_ffn_expert_bias': _L3_ffn_in['expert_bias'], 'L3_ffn_sw1': _L3_ffn_in['sw1'], 'L3_ffn_sw2': _L3_ffn_in['sw2'], 'L3_ffn_sw3': _L3_ffn_in['sw3']}

def reference(x, fside_S2_0, ctx_2048, mask_BxS2_ik0, mask_BxSxS2_ff0, g_xattn, g_ffn, L0_xattn_k, L0_ffn_gate_w, L0_ffn_w_gate, L0_ffn_w_up, L0_ffn_w_down, L1_xattn_Wq, L1_xattn_bq, L1_xattn_Wk, L1_xattn_bk, L1_xattn_Wv, L1_xattn_bv, L1_xattn_Wo, L1_xattn_bo, L1_xattn_ln_gamma, L1_xattn_ln_beta, L1_xattn_residual_scale, L1_ffn_W_gate, L1_ffn_W_qkv, L2_xattn_wq, L2_xattn_wk, L2_xattn_wv, L2_xattn_wo, L2_xattn_wk_ctx, L2_xattn_wv_ctx, L2_xattn_q_norm_w, L2_xattn_k_norm_w, L2_ffn_gate_w, L2_ffn_gate_b, L2_ffn_val_w, L2_ffn_val_b, L2_ffn_out_w, L2_ffn_out_b, L3_xattn_wq, L3_xattn_bq, L3_xattn_wk, L3_xattn_bk, L3_xattn_wv, L3_xattn_bv, L3_xattn_wo, L3_xattn_bo, L3_ffn_w12, L3_ffn_w3, L3_ffn_router_w, L3_ffn_expert_bias, L3_ffn_sw1, L3_ffn_sw2, L3_ffn_sw3):
    import jax
    import jax.numpy as jnp

    def _L0_xattn_ref(v, k, bias, x1, x2, num_heads):
        import jax, jax.numpy as jnp
        import numpy as np
        B, D, L = v.shape
        H = D // num_heads
        fft_size = 2 * L
        vr = v.reshape(B, H, num_heads, L)
        x1r = x1.reshape(B, H, num_heads, L)
        x2r = x2.reshape(B, H, num_heads, L)
        kv = vr[:, :, :, None, :] * x2r[:, :, None, :, :]
        k_f = jnp.fft.rfft(k.astype(jnp.float32), n=fft_size)
        y = jnp.fft.irfft(jnp.fft.rfft(kv, n=fft_size) * k_f[None, :, None, None, :], n=fft_size)[..., :L]
        skip = bias.astype(jnp.float32).reshape(H, num_heads)[None, :, :, None, None]
        y = y + kv * skip
        out = jnp.einsum('bhijl,bhil->bhjl', y, x1r)
        return out.reshape(B, D, L)

    def _L0_ffn_ref(hidden_states, gate_w, w_gate, w_up, w_down):
        import jax, jax.numpy as jnp
        import numpy as np
        HIDDEN = 256
        INTER = 96
        N_EXPERTS = 32
        TOP_K = 8
        B, S, H = hidden_states.shape
        E = gate_w.shape[1]
        x = hidden_states.reshape(-1, H)
        T = x.shape[0]
        K = TOP_K
        P = T * K
        C = 2 * (P // E)
        probs = jax.nn.softmax(x @ gate_w, axis=-1)
        w, sel = jax.lax.top_k(probs, K)
        w = w / jnp.sum(w, axis=-1, keepdims=True)
        flat_e = sel.reshape(-1)
        flat_t = jnp.repeat(jnp.arange(T), K)
        flat_w = w.reshape(-1)
        order = jnp.argsort(flat_e)
        se = flat_e[order]
        start = jnp.searchsorted(se, jnp.arange(E))
        pos = jnp.arange(P) - start[se]
        slot = jnp.where(pos < C, se * C + pos, E * C)
        slot_pair = jnp.full((E * C,), P, dtype=jnp.int32).at[slot].set(order.astype(jnp.int32), mode='drop')
        t_slot = jnp.concatenate([flat_t, jnp.array([T])])[slot_pair]
        w_slot = jnp.concatenate([flat_w, jnp.zeros((1,), flat_w.dtype)])[slot_pair]
        x_pad = jnp.concatenate([x, jnp.zeros((1, H), x.dtype)], axis=0)
        xg = x_pad[t_slot].reshape(E, C, H)
        g = jnp.einsum('ech,ehi->eci', xg, w_gate)
        u = jnp.einsum('ech,ehi->eci', xg, w_up)
        y = jnp.einsum('eci,eih->ech', jax.nn.silu(g) * u, w_down).reshape(E * C, H)
        out = jnp.zeros((T + 1, H), x.dtype).at[t_slot].add(w_slot[:, None] * y)
        return out[:T].reshape(B, S, H)

    def _L1_xattn_ref(hidden_states, audio_tokens, attention_mask, Wq, bq, Wk, bk, Wv, bv, Wo, bo, ln_gamma, ln_beta, residual_scale):
        import jax, jax.numpy as jnp
        import numpy as np
        import math
        H = 256
        NH = 16
        HD = H // NH
        EPS_LN = 1e-05
        RES_SCALE_MAX = 0.3

        def _nan_clean(x, lim=10000.0):
            return jnp.nan_to_num(x, nan=0.0, posinf=lim, neginf=-lim)
        B, S, _ = hidden_states.shape
        T = audio_tokens.shape[1]
        hs = _nan_clean(hidden_states).astype(jnp.float32)
        at = _nan_clean(audio_tokens).astype(jnp.float32)

        def proj(x, W, b, L):
            y = x @ W.T + b
            return y.reshape(B, L, NH, HD).transpose(0, 2, 1, 3)
        q = _nan_clean(proj(hs, Wq, bq, S))
        k = _nan_clean(proj(at, Wk, bk, T))
        v = _nan_clean(proj(at, Wv, bv, T))
        scale = max(math.sqrt(HD), 1e-08)
        scores = jnp.einsum('bhsd,bhtd->bhst', q, k) / scale
        scores = jnp.clip(scores, -50.0, 50.0)
        scores = jnp.nan_to_num(scores, nan=0.0, posinf=50.0, neginf=-50.0)
        attend = (attention_mask.astype(jnp.float32) > 0.5)[:, None, None, :]
        scores = jnp.where(attend, scores, -10000.0)
        scores = jnp.clip(scores, -50.0, 50.0)
        probs = jax.nn.softmax(scores, axis=-1)
        probs = jnp.nan_to_num(probs, nan=0.0, posinf=1.0, neginf=0.0)
        probs = probs / (probs.sum(axis=-1, keepdims=True) + 1e-08)
        ctx = jnp.einsum('bhst,bhtd->bhsd', probs, v)
        ctx = ctx.transpose(0, 2, 1, 3).reshape(B, S, H)
        delta = _nan_clean(ctx @ Wo.T + bo)
        rs = jnp.clip(residual_scale, 0.0, RES_SCALE_MAX)
        delta = rs * delta
        mu = delta.mean(axis=-1, keepdims=True)
        var = jnp.mean((delta - mu) ** 2, axis=-1, keepdims=True)
        delta = (delta - mu) / jnp.sqrt(var + EPS_LN) * ln_gamma + ln_beta
        return delta

    def _L1_ffn_ref(x, W_gate, W_qkv):
        import jax, jax.numpy as jnp
        import numpy as np
        import math
        N_EMBD = 256
        N_HEAD = 16
        HEAD_DIM = N_EMBD // N_HEAD
        B, T = (2, 256)
        Bb, Tt, C = x.shape
        H, hd = (N_HEAD, HEAD_DIM)
        gating = jax.nn.softmax(x @ W_gate.T, axis=-1)
        idx = jnp.argmax(gating, axis=-1)
        indicator = jax.nn.one_hot(idx, H, dtype=gating.dtype)
        top1_val = jnp.max(gating, axis=-1, keepdims=True)
        gating_top1 = indicator * top1_val
        qkv = x @ W_qkv.T
        q, k, v = jnp.split(qkv, 3, axis=-1)
        k = k.reshape(Bb, Tt, H, hd)
        v = v.reshape(Bb, Tt, H, hd)
        k_shared = jnp.einsum('bth,bthd->btd', indicator, k)
        v_shared = jnp.einsum('bth,bthd->btd', gating_top1, v)
        q = q.reshape(Bb, Tt, H, hd).transpose(0, 2, 1, 3)
        att = jnp.einsum('bhqd,bkd->bhqk', q, k_shared) * (1.0 / math.sqrt(hd))
        causal = jnp.tril(jnp.ones((Tt, Tt), dtype=bool))
        att = jnp.where(causal[None, None, :, :], att, -jnp.inf)
        att = jax.nn.softmax(att, axis=-1)
        y = jnp.einsum('bhqk,bkd->bhqd', att, v_shared)
        y = y.transpose(0, 2, 1, 3).reshape(Bb, Tt, C)
        return y

    def _L2_xattn_ref(x, h_ctx_kv, wq, wk, wv, wo, wk_ctx, wv_ctx, q_norm_w, k_norm_w):
        import jax, jax.numpy as jnp
        import numpy as np
        HIDDEN = 256
        NUM_HEADS = 16
        NUM_KV_HEADS = 4
        HEAD_DIM = 128
        ROPE_THETA = 10000.0
        EPS = 1e-06

        def rms_norm(x, w, eps=EPS):
            var = jnp.mean(jnp.square(x), axis=-1, keepdims=True)
            return x * jax.lax.rsqrt(var + eps) * w

        def rope_cache(L, head_dim, theta, dtype):
            inv_freq = 1.0 / theta ** (jnp.arange(0, head_dim, 2, dtype=jnp.float32) / head_dim)
            t = jnp.arange(L, dtype=jnp.float32)
            freqs = jnp.outer(t, inv_freq)
            emb = jnp.concatenate([freqs, freqs], -1)
            cos = jnp.cos(emb).astype(dtype)[None, :, None, :]
            sin = jnp.sin(emb).astype(dtype)[None, :, None, :]
            return (cos, sin)

        def rotate_half(x):
            x1, x2 = jnp.split(x, 2, axis=-1)
            return jnp.concatenate([-x2, x1], axis=-1)
        B, L, _ = x.shape
        T = h_ctx_kv.shape[1]
        rep = NUM_HEADS // NUM_KV_HEADS
        q = (x @ wq).reshape(B, L, NUM_HEADS, HEAD_DIM)
        k = (x @ wk).reshape(B, L, NUM_KV_HEADS, HEAD_DIM)
        v = (x @ wv).reshape(B, L, NUM_KV_HEADS, HEAD_DIM)
        q = rms_norm(q, q_norm_w)
        k = rms_norm(k, k_norm_w)
        k_ctx = (h_ctx_kv @ wk_ctx).reshape(B, T, NUM_KV_HEADS, HEAD_DIM)
        v_ctx = (h_ctx_kv @ wv_ctx).reshape(B, T, NUM_KV_HEADS, HEAD_DIM)
        k_ctx = rms_norm(k_ctx, k_norm_w)
        cos, sin = rope_cache(L, HEAD_DIM, ROPE_THETA, x.dtype)
        q = q * cos + rotate_half(q) * sin
        k = k * cos + rotate_half(k) * sin
        k_full = jnp.concatenate([k_ctx, k], axis=1)
        v_full = jnp.concatenate([v_ctx, v], axis=1)
        k_full = jnp.repeat(k_full, rep, axis=2)
        v_full = jnpp_repeat = jnp.repeat(v_full, rep, axis=2)
        i = jnp.arange(L)[:, None]
        j = jnp.arange(L)[None, :]
        causal = jnp.where(j > i, -jnp.inf, 0.0).astype(x.dtype)
        mask = jnp.concatenate([jnp.zeros((L, T), x.dtype), causal], axis=1)
        scale = 1.0 / np.sqrt(HEAD_DIM)
        scores = jnp.einsum('blhd,bmhd->bhlm', q, k_full) * scale + mask
        probs = jax.nn.softmax(scores, axis=-1)
        out = jnp.einsum('bhlm,bmhd->blhd', probs, v_full)
        out = out.reshape(B, L, NUM_HEADS * HEAD_DIM)
        return out @ wo

    def _L2_ffn_ref(x, gate_w, gate_b, val_w, val_b, out_w, out_b):
        import jax, jax.numpy as jnp
        import numpy as np
        D_MODEL = 256
        HIDDEN = 4 * D_MODEL
        B, S = (2, 512)

        def bit_linear(x, w, b):
            gamma_x = jnp.clip(jnp.max(jnp.abs(x), axis=-1, keepdims=True), 1e-05, None)
            scale_x = 127.0 / gamma_x
            x_dq = jnp.clip(jnp.round(x * scale_x), -128.0, 127.0) / scale_x
            x_ste = x + jax.lax.stop_gradient(x_dq - x)
            gamma_w = jnp.clip(jnp.mean(jnp.abs(w)), 1e-05, None)
            w_dq = jnp.clip(jnp.round(w / gamma_w), -1.0, 1.0) * gamma_w
            w_ste = w + jax.lax.stop_gradient(w_dq - w)
            return jnp.einsum('bsd,hd->bsh', x_ste, w_ste) + b
        gate = jax.nn.silu(bit_linear(x, gate_w, gate_b))
        val = bit_linear(x, val_w, val_b)
        return bit_linear(gate * val, out_w, out_b)

    def _L3_xattn_ref(x, cond, mask, wq, bq, wk, bk, wv, bv, wo, bo):
        import jax, jax.numpy as jnp
        import numpy as np
        NUM_HEADS = 16
        EPS = 1e-08

        def _dyn_quant(x):
            s = jnp.maximum(jnp.max(jnp.abs(x), axis=-1, keepdims=True) / 127.0, EPS)
            q = jnp.clip(jnp.round(x / s), -127.0, 127.0)
            return (q, s)

        def _quant_weight(w):
            s = jnp.maximum(jnp.max(jnp.abs(w), axis=1, keepdims=True) / 127.0, EPS)
            q = jnp.clip(jnp.round(w / s), -127.0, 127.0)
            return (q, s)

        def _w8a8_linear(x, w, b):
            qx, sx = _dyn_quant(x)
            qw, sw = _quant_weight(w)
            y = jnp.einsum('bnc,oc->bno', qx, qw) * (sx * sw[:, 0])
            return y + b
        B, N, C = x.shape
        L = cond.shape[1]
        H = NUM_HEADS
        D = C // H
        inv_sqrt_d = np.float32(1.0 / np.sqrt(D))
        q = _w8a8_linear(x, wq, bq).reshape(B, N, H, D).transpose(0, 2, 1, 3)
        k = (cond @ wk.T + bk).reshape(B, L, H, D).transpose(0, 2, 1, 3)
        v = (cond @ wv.T + bv).reshape(B, L, H, D).transpose(0, 2, 1, 3)
        scores = jnp.einsum('bhnd,bhld->bhnl', q, k) * inv_sqrt_d + mask[:, None]
        attn = jax.nn.softmax(scores, axis=-1)
        o = jnp.einsum('bhnl,bhld->bhnd', attn, v)
        o = o.transpose(0, 2, 1, 3).reshape(B, N, C)
        return _w8a8_linear(o, wo, bo)

    def _L3_ffn_ref(x, w12, w3, router_w, expert_bias, sw1, sw2, sw3):
        import jax, jax.numpy as jnp
        import numpy as np
        B, S, D = (2, 256, 256)
        E = 8
        TOPK = 2
        H_SHARED = 1024
        H_ROUTED = 128
        STD = 0.02
        b, s, d = x.shape
        g = x @ sw1.T
        u = x @ sw2.T
        shared_out = jax.nn.silu(g) * u @ sw3.T
        scores = jax.nn.sigmoid(x @ router_w.T)
        selection_scores = scores + expert_bias
        _, top_idx = jax.lax.top_k(selection_scores, TOPK)
        top_scores = jnp.take_along_axis(scores, top_idx, axis=-1)
        top_scores = top_scores / (top_scores.sum(-1, keepdims=True) + 1e-09)
        flat_x = x.reshape(-1, d)
        T = flat_x.shape[0]
        flat_idx = top_idx.reshape(T, TOPK)
        flat_sc = top_scores.reshape(T, TOPK)
        combine = jnp.zeros((T, E), x.dtype).at[jnp.arange(T)[:, None], flat_idx].add(flat_sc)
        h12 = jnp.einsum('td,ehd->teh', flat_x, w12)
        h1, h2 = jnp.split(h12, 2, axis=-1)
        h = jax.nn.silu(h1) * h2
        out_e = jnp.einsum('teh,edh->ted', h, w3)
        routed_out = jnp.einsum('ted,te->td', out_e, combine).reshape(b, s, d)
        return shared_out + routed_out
    x = x + jnp.tanh(g_xattn[0]) * _L0_xattn_ref(_layernorm(x, axis=-1), L0_xattn_k, fside_S2_0, ctx_2048, ctx_2048, 8)
    x = x + jnp.tanh(g_ffn[0]) * _L0_ffn_ref(_layernorm(x, axis=-1), L0_ffn_gate_w, L0_ffn_w_gate, L0_ffn_w_up, L0_ffn_w_down)
    x = x + jnp.tanh(g_xattn[1]) * _L1_xattn_ref(_layernorm(x, axis=-1), ctx_2048, mask_BxS2_ik0, L1_xattn_Wq, L1_xattn_bq, L1_xattn_Wk, L1_xattn_bk, L1_xattn_Wv, L1_xattn_bv, L1_xattn_Wo, L1_xattn_bo, L1_xattn_ln_gamma, L1_xattn_ln_beta, L1_xattn_residual_scale)
    x = x + jnp.tanh(g_ffn[1]) * _L1_ffn_ref(_layernorm(x, axis=-1), L1_ffn_W_gate, L1_ffn_W_qkv)
    x = x + jnp.tanh(g_xattn[2]) * _L2_xattn_ref(_layernorm(x, axis=-1), ctx_2048, L2_xattn_wq, L2_xattn_wk, L2_xattn_wv, L2_xattn_wo, L2_xattn_wk_ctx, L2_xattn_wv_ctx, L2_xattn_q_norm_w, L2_xattn_k_norm_w)
    x = x + jnp.tanh(g_ffn[2]) * _L2_ffn_ref(_layernorm(x, axis=-1), L2_ffn_gate_w, L2_ffn_gate_b, L2_ffn_val_w, L2_ffn_val_b, L2_ffn_out_w, L2_ffn_out_b)
    x = x + jnp.tanh(g_xattn[3]) * _L3_xattn_ref(_layernorm(x, axis=-1), ctx_2048, mask_BxSxS2_ff0, L3_xattn_wq, L3_xattn_bq, L3_xattn_wk, L3_xattn_bk, L3_xattn_wv, L3_xattn_bv, L3_xattn_wo, L3_xattn_bo)
    x = x + jnp.tanh(g_ffn[3]) * _L3_ffn_ref(_layernorm(x, axis=-1), L3_ffn_w12, L3_ffn_w3, L3_ffn_router_w, L3_ffn_expert_bias, L3_ffn_sw1, L3_ffn_sw2, L3_ffn_sw3)
    return x

_drawn_inputs = setup_inputs


def setup_inputs(seed=0):
    import zlib

    import numpy as np

    out = dict(_drawn_inputs(seed))
    spreads = {'L1_xattn_bq': (0.0, 0.737),
     'L1_xattn_bk': (0.0, 0.8),
     'L1_xattn_bv': (0.0, 0.1),
     'L1_xattn_bo': (0.0, 0.1),
     'L1_xattn_ln_gamma': (1.0, 0.2),
     'L1_xattn_ln_beta': (0.0, 0.326),
     'L2_xattn_q_norm_w': (1.0, 0.6),
     'L2_xattn_k_norm_w': (1.0, 0.6),
     'L2_ffn_gate_b': (0.0, 0.8),
     'L2_ffn_val_b': (0.0, 0.8),
     'L2_ffn_out_b': (0.0, 0.417),
     'L3_xattn_bq': (0.0, 0.8),
     'L3_xattn_bk': (0.0, 0.8),
     'L3_xattn_bv': (0.0, 0.8),
     'L3_xattn_bo': (0.0, 0.426),
     'L3_ffn_expert_bias': (0.0, 0.8)}
    factors = {'g_ffn': 8.0,
     'L1_ffn_W_gate': 8.0,
     'L1_ffn_W_qkv': 8.0,
     'L2_xattn_wk': 3.557,
     'L2_ffn_gate_w': 8.0,
     'L2_ffn_val_w': 8.0,
     'L2_ffn_out_w': 8.0,
     'L3_xattn_wq': 8.0,
     'L3_xattn_wk': 8.0,
     'L3_xattn_wv': 5.611,
     'L3_xattn_wo': 4.832,
     'L3_ffn_w12': 8.0,
     'L3_ffn_w3': 8.0,
     'L3_ffn_router_w': 8.0,
     'L3_ffn_sw1': 7.88,
     'L3_ffn_sw2': 7.764,
     'L3_ffn_sw3': 7.767}
    for name, (base, spread) in spreads.items():
        noise = np.random.default_rng([zlib.crc32(name.encode()), seed]).standard_normal(out[name].shape)
        drawn = base * np.exp(spread * noise) if base else spread * noise
        out[name] = jnp.asarray(drawn.astype(out[name].dtype))
    for name, factor in factors.items():
        out[name] = (out[name] * factor).astype(out[name].dtype)
    return out
```

```python
from contextlib import ExitStack

import concourse.bass as bass
import numpy as np
from concourse import mybir

UPTO = 8

ALU = mybir.AluOpType
ACT = mybir.ActivationFunctionType
AX = mybir.AxisListType
F32 = mybir.dt.float32
BF16 = mybir.dt.bfloat16
I32 = mybir.dt.int32
U16 = mybir.dt.uint16

B, P, C = 16, 128, 256
KC = C // P
NH, HD = 16, 16
SLOT = 32
NEG = -1.0e30
ROUND = 12582912.0
LN_EPS = 1e-5


def bc(ap, n):
    return ap.unsqueeze(2).to_broadcast([ap.shape[0], ap.shape[1], n])


def heads(ap, n=NH):
    return ap.rearrange("p (h d) -> p h d", h=n)


class Chain:

    def __init__(self, eng, sem, per):
        self.eng, self.sem, self.per, self.base, self.n = eng, sem, per, None, per

    def turn(self, b):
        assert self.n == self.per, (self.sem, self.n, self.per)
        self.base, self.n = b * self.per, 0

    def __call__(self, ins):
        self.n += 1
        ins.then_inc(self.sem, 1)
        self.eng.wait_ge(self.sem, self.base + self.n)


def sweep(eng, front, body):
    front(0, 0)
    front(1, 1)
    body(0, 0)
    with eng.Fori(1, B // 2) as i:
        front(2 * i, 0)
        body(2 * i - 1, 1)
        front(2 * i + 1, 1)
        body(2 * i, 0)
    body(B - 1, 1)


def hold(eng, sem, v, spare):
    eng.wait_ge(sem, v)
    eng.sem_inc(spare, 1)


def after(eng, sem, v):
    if not (isinstance(v, int) and v <= 0):
        eng.wait_ge(sem, v)


class Phase:

    def __init__(self, nc, name):
        self.nc, self.name, self.ctx, self.sems = nc, name, ExitStack(), []

    def __enter__(self):
        self.ctx.__enter__()
        return self

    def __exit__(self, *a):
        self.ctx.__exit__(*a)
        if self.sems:
            self.nc.clear_and_free_semaphores(self.sems)
            self.nc.all_engine_barrier(sem_only=True)

    def sem(self, name):
        self.sems.append(self.nc.alloc_semaphore(f"{self.name}_{name}"))
        return self.sems[-1]

    def sb(self, name, shape, dt=F32):
        return self.ctx.enter_context(self.nc.sbuf_tensor(f"{self.name}_{name}", shape, dt))

    def ps(self, name, dt=F32):
        cols = 512 if dt == F32 else 1024
        return self.ctx.enter_context(self.nc.psum_tensor(f"{self.name}_{name}", [P, cols], dt))

    def block(self):
        return self.ctx.enter_context(self.nc.Block())


class Norm:

    def __init__(self, ph, G, ps):
        self.G, self.ps = G, ps
        self.stat_steps, self.stats_ready, self.rstd_steps, self.xn_ready, self.xT_ps, self.xT_ready = (
            ph.sem(n) for n in ("stat_steps", "stats_ready", "rstd_steps", "xn_ready", "xT_ps", "xT_ready"))
        self.stats = ph.sb("ln_stats", [P, 6])
        self.mv = [ph.sb(f"ln_mv{i}", [P, 2]) for i in range(2)]
        self.rstd = [ph.sb(f"ln_rstd{i}", [P, 1]) for i in range(2)]
        self.xn = [ph.sb(f"xn{i}", [P, C]) for i in range(2)]
        self.xT = [ph.sb(f"xT{i}", [P, KC, P]) for i in range(2)]

    def vector(self, dve, b, p):
        if not (isinstance(b, int) and b < 2):
            dve.wait_ge(self.xn_ready, b - 1)
        dve.bn_stats(self.stats[:], self.G["x_all"][:, b, :]).then_inc(self.stat_steps, 1)
        hold(dve, self.stat_steps, b + 1, self.G["spare"])
        dve.bn_aggr(self.mv[p][:], self.stats[:]).then_inc(self.stats_ready, 1)

    def pool(self, pool, b, p):
        pool.wait_ge(self.stats_ready, b + 1)
        pool.tensor_tensor(self.rstd[p][:], self.mv[p][:, 1:2], self.G["eps"][:, 0:1],
                           ALU.add).then_inc(self.rstd_steps, 1)
        pool.wait_ge(self.rstd_steps, 2 * b + 1)
        pool.tensor_tensor(self.rstd[p][:], self.rstd[p][:], self.G["minus_half"][:, 0:1],
                           ALU.pow).then_inc(self.rstd_steps, 1)

    def normalise(self, dve, b, p):
        dve.wait_ge(self.rstd_steps, 2 * b + 2)
        if self.ps is not None:
            after(dve, self.xT_ps, b - 1)
        dve.tensor_scalar(self.xn[p][:], self.G["x_all"][:, b, :], self.mv[p][:, 0:1], self.rstd[p][:, 0:1],
                          ALU.subtract, ALU.mult).then_inc(self.xn_ready, 1)

    def front(self, dve, b, p):
        self.vector(dve, b, p)
        self.normalise(dve, b, p)

    def tensor(self, pe, b, p):
        after(pe, self.xT_ready, b)
        pe.wait_ge(self.xn_ready, b + 1)
        for k in range(KC):
            last = pe.transpose(self.ps[:, k * P:(k + 1) * P], self.xn[p][:, k * P:(k + 1) * P],
                                self.G["ident"][:])
        last.then_inc(self.xT_ps, 1)

    def scalar(self, act, b, p):
        act.wait_ge(self.xT_ps, b + 1)
        act.activation(self.xT[p][:].rearrange("p k t -> p (k t)"), self.ps[:, 0:C],
                       ACT.Copy).then_inc(self.xT_ready, 1)


def phase_setup(nc, D, G):
    with Phase(nc, "setup") as ph:
        loaded = ph.sem("loaded")
        g_raw = ph.sb("g_raw", [P, 8])
        done = ph.sem("done")
        block = ph.block()
        n = [0]

        @block.sync
        def _(sp):
            def load(dst, src):
                n[0] += 16
                sp.dma_start(dst, src).then_inc(loaded, 16)

            load(g_raw[:, 0:4], D["g_xattn"].partition_broadcast(P))
            load(g_raw[:, 4:8], D["g_ffn"].partition_broadcast(P))
            load(G["ident"][:], D["c_ident"])
            load(G["identb"][:].bitcast(U16), D["c_identb"])
            load(G["minus_half"][:], D["c_minus_half"])
            load(G["eps"][:], D["c_eps"])
            load(G["x_all"][:], D["x"].rearrange("b t c -> t b c"))
            sp.wait_ge(loaded, n[0])

        @block.scalar
        def _(act):
            act.wait_ge(loaded, n[0])
            act.activation(G["tg"][:], g_raw[:], ACT.Tanh).then_inc(done, 1)


def phase_hyena(nc, D, G):
    HG, HI = 16, 8
    with Phase(nc, "hyena") as ph:
        vT = ph.sb("vT", [P, KC, B * P])
        aT = ph.sb("aT", [P, KC, B * P])
        ctxT, x_all, tg = G["ctxT"], G["x_all"], G["tg"]

        with Phase(nc, "hyA") as pa:
            pT, pD = pa.ps("pT"), pa.ps("pD")
            nm = Norm(pa, G, pT)
            xn = nm.xn
            ctx = [pa.sb(f"ctx{i}", [P, C]) for i in range(2)]
            m1 = [pa.sb(f"m1{i}", [P, C]) for i in range(2)]
            skip = [pa.sb(f"skip{i}", [P, C]) for i in range(2)]
            blockones = pa.sb("blockones", [P, P])
            biascol = pa.sb("biascol", [P, 1])
            gmat = pa.sb("gmat", [P, P])
            const_in, gmat_ready, m1_ready, skip_ps, evac, added = (
                pa.sem(n) for n in ("const_in", "gmat_ready", "m1_ready", "skip_ps", "evac", "added"))
            ctx_in = [pa.sem(f"ctx_in{i}") for i in range(2)]
            block = pa.block()

            @block.sync
            def _(sp):
                sp.dma_start(blockones[:], D["c_blockones"]).then_inc(const_in, 16)
                sp.dma_start(biascol[:], D["fside_S2_0"].rearrange("(p a) -> p a", a=1)).then_inc(const_in, 16)
                for p in range(2):
                    sp.dma_start(ctx[p][:], D["ctx_2048"][p]).then_inc(ctx_in[p], 16)
                with sp.Fori(0, B // 2 - 1) as i:
                    for p in range(2):
                        sp.wait_ge(added, 2 * i + p + 1)
                        sp.wait_ge(nm.xT_ps, 2 * i + p + 1)
                        sp.dma_start(ctx[p][:], D["ctx_2048"][2 * i + 2 + p]).then_inc(ctx_in[p], 16)
                G["load"](sp, "moe")
                G["load"](sp, "small")

            @block.gpsimd
            def _(pool):
                sweep(pool, lambda b, p: nm.pool(pool, b, p), lambda b, p: None)

            @block.vector
            def _(dve):
                dve.wait_ge(const_in, 32)
                dve.tensor_scalar(gmat[:], blockones[:], biascol[:, 0:1], None, ALU.mult).then_inc(gmat_ready, 1)

                def body(b, p):
                    x = x_all[:, b, :]
                    dve.wait_ge(nm.xn_ready, b + 1)
                    dve.wait_ge(ctx_in[p], 8 * (b - p) + 16)
                    dve.tensor_tensor(m1[p][:], xn[p][:], ctx[p][:], ALU.mult).then_inc(m1_ready, 1)
                    dve.wait_ge(skip_ps, b + 1)
                    dve.tensor_tensor(skip[p][:], pD[:, p * C:(p + 1) * C], ctx[p][:], ALU.mult).then_inc(added, 1)
                    dve.wait_ge(added, b + 1)
                    dve.scalar_tensor_tensor(x, skip[p][:], tg[:, 0:1], x, ALU.mult, ALU.add)

                sweep(dve, lambda b, p: nm.front(dve, b, p), body)

            @block.tensor
            def _(pe):
                pe.wait_ge(gmat_ready, 1)

                def body(b, p):
                    pe.wait_ge(m1_ready, b + 1)
                    pe.wait_ge(ctx_in[p], 8 * (b - p) + 16)
                    after(pe, evac, 2 * b)
                    for k in range(KC):
                        pe.transpose(pT[:, k * P:(k + 1) * P], xn[p][:, k * P:(k + 1) * P], G["ident"][:])
                    for k in range(KC):
                        last = pe.transpose(pT[:, C + k * P:C + (k + 1) * P], ctx[p][:, k * P:(k + 1) * P],
                                            G["ident"][:])
                    last.then_inc(nm.xT_ps, 1)
                    pe.matmul(pD[:, p * C:(p + 1) * C], lhsT=gmat[:], rhs=m1[p][:], start=True,
                              stop=True).then_inc(skip_ps, 1)

                body(0, 0)
                body(1, 1)
                with pe.Fori(1, B // 2) as i:
                    body(2 * i, 0)
                    body(2 * i + 1, 1)

            @block.scalar
            def _(act):
                with act.Fori(0, B) as b:
                    act.wait_ge(nm.xT_ps, b + 1)
                    act.activation(vT[:, :, bass.ds(b * P, P)], pT[:, 0:C].rearrange("p (k t) -> p k t", k=KC),
                                   ACT.Copy).then_inc(evac, 1)
                    act.activation(ctxT[:, :, bass.ds(b * P, P)], pT[:, C:2 * C].rearrange("p (k t) -> p k t", k=KC),
                                   ACT.Copy).then_inc(evac, 1)

        with Phase(nc, "hyB") as pb:
            NB2 = B // 2
            toep_rev = [pb.sb(f"toep_rev{i}", [P, C]) for i in range(2)]
            toep = [pb.sb(f"toep{i}", [P, C]) for i in range(2)]
            prod = [pb.sb(f"prod{i}", [P, KC, B * HI * HI]) for i in range(2)]
            gated = [pb.sb(f"gated{i}", [P, NB2 * HI * HI]) for i in range(2)]
            bank = [[pb.ps(f"y{i}{j}") for j in range(4)] for i in range(2)]
            toep_in = [pb.sem(f"toep_in{i}") for i in range(2)]
            toep_ready, prod_ready, conv_ps, gate_steps, summed = (
                pb.sem(n) for n in ("toep_ready", "prod_ready", "conv_ps", "gate_steps", "summed"))
            block = pb.block()

            def group(t, c, h, b0, n):
                v = t[:, c, :].rearrange("p (b g i) -> p b g i", g=HG, i=HI)
                return v[:, b0:b0 + n, h, :]

            @block.sync
            def _(sp):
                kp = D["k_rev"]

                def load(h, p):
                    src = bass.AP(kp.tensor, h * kp.shape[1], [[1, P], [1, C]])
                    sp.dma_start(toep_rev[p][:], src).then_inc(toep_in[p], 16)

                load(0, 0)
                load(1, 1)
                with sp.Fori(0, HG // 2 - 1) as i:
                    for p in range(2):
                        sp.wait_ge(toep_ready, 2 * i + p + 1)
                        load(2 * i + 2 + p, p)

            @block.scalar
            def _(act):
                def turn(i, p):
                    act.wait_ge(toep_in[p], 16 * i + 16)
                    act.activation(toep[p][:], toep_rev[p][:, ::-1], ACT.Copy).then_inc(toep_ready, 1)

                turn(0, 0)
                turn(0, 1)
                with act.Fori(1, HG // 2) as i:
                    for p in range(2):
                        act.wait_ge(conv_ps, 4 * (2 * i + p - 1))
                        turn(i, p)

            @block.gpsimd
            def _(pool):
                def turn(i, p):
                    h = 2 * i + p
                    for c in range(KC):
                        v = group(vT, c, h, 0, B).unsqueeze(3).to_broadcast([P, B, HI, HI])
                        x2 = group(ctxT, c, h, 0, B).unsqueeze(2).to_broadcast([P, B, HI, HI])
                        out = prod[p][:, c, :].rearrange("p (b i j) -> p b i j", i=HI, j=HI)
                        pool.tensor_tensor(out, v, x2, ALU.mult).then_inc(prod_ready, 1)

                turn(0, 0)
                turn(0, 1)
                with pool.Fori(1, HG // 2) as i:
                    for p in range(2):
                        pool.wait_ge(conv_ps, 4 * (2 * i + p - 1))
                        turn(i, p)

            @block.tensor
            def _(pe):
                def turn(i, p, first):
                    h = 2 * i + p
                    pe.wait_ge(toep_ready, h + 1)
                    for c in range(KC):
                        pe.wait_ge(prod_ready, 2 * h + c + 1)
                        for n in range(2):
                            if not first:
                                pe.wait_ge(gate_steps, 4 * (h - 2) + 2 * c + n + 1)
                            y = bank[p][2 * c + n]
                            cols = slice(n * 512, n * 512 + 512)
                            if c == 1:
                                pe.matmul(y[:], lhsT=toep[p][:, P:C], rhs=prod[p][:, 0, cols], start=True, stop=False)
                            pe.matmul(y[:], lhsT=toep[p][:, 0:P], rhs=prod[p][:, c, cols], start=(c == 0),
                                      stop=True).then_inc(conv_ps, 1)

                turn(0, 0, True)
                turn(0, 1, True)
                with pe.Fori(1, HG // 2) as i:
                    turn(i, 0, False)
                    turn(i, 1, False)

            @block.vector
            def _(dve):
                with dve.Fori(0, HG // 2) as i:
                    for p in range(2):
                        h = 2 * i + p
                        for c in range(KC):
                            for n in range(2):
                                q = 4 * h + 2 * c + n
                                g = gated[n][:].rearrange("p (b i j) -> p b i j", i=HI, j=HI)
                                x1 = group(ctxT, c, h, n * NB2, NB2).unsqueeze(3).to_broadcast([P, NB2, HI, HI])
                                y = bank[p][2 * c + n][:].rearrange("p (b i j) -> p b i j", i=HI, j=HI)
                                dve.wait_ge(conv_ps, q + 1)
                                dve.tensor_tensor(g, y, x1, ALU.mult).then_inc(gate_steps, 1)
                                dve.wait_ge(gate_steps, q + 1)
                                dve.tensor_reduce(group(aT, c, h, n * NB2, NB2),
                                                  gated[n][:].rearrange("p (b i j) -> p b j i", i=HI, j=HI),
                                                  AX.X, ALU.add).then_inc(summed, 1)
                                dve.wait_ge(summed, q + 1)

        with Phase(nc, "hyC") as pc:
            slot = [pc.sb(f"slot{i}", [P, KC, P]) for i in range(2)]
            pB = [pc.ps(f"pB{i}") for i in range(2)]
            copied, back_ps, added = (pc.sem(n) for n in ("copied", "back_ps", "added"))
            block = pc.block()

            @block.scalar
            def _(act):
                def turn(i, p, first):
                    b = 2 * i + p
                    if not first:
                        act.wait_ge(back_ps, b - 1)
                    act.activation(slot[p][:], aT[:, :, bass.ds(b * P, P)], ACT.Copy).then_inc(copied, 1)

                turn(0, 0, True)
                turn(0, 1, True)
                with act.Fori(1, B // 2) as i:
                    turn(i, 0, False)
                    turn(i, 1, False)

            @block.tensor
            def _(pe):
                def turn(i, p, first):
                    b = 2 * i + p
                    pe.wait_ge(copied, b + 1)
                    if not first:
                        pe.wait_ge(added, b - 1)
                    for k in range(KC):
                        last = pe.transpose(pB[p][:, k * P:(k + 1) * P], slot[p][:, k, :], G["ident"][:])
                    last.then_inc(back_ps, 1)

                turn(0, 0, True)
                turn(0, 1, True)
                with pe.Fori(1, B // 2) as i:
                    turn(i, 0, False)
                    turn(i, 1, False)

            @block.vector
            def _(dve):
                with dve.Fori(0, B // 2) as i:
                    for p in range(2):
                        b = 2 * i + p
                        dve.wait_ge(back_ps, b + 1)
                        dve.scalar_tensor_tensor(x_all[:, b, :], pB[p][:, 0:C], tg[:, 0:1], x_all[:, b, :],
                                                 ALU.mult, ALU.add).then_inc(added, 1)


def gated_mlp(nc, G, name, gate, w_gate, w_up, w_down, hidden, chunk, weights, loaded):
    NC, KT = hidden // chunk, chunk // P
    weighted = [weights(0, c) is not None for c in range(NC)]
    NW = sum(weighted)
    with Phase(nc, name) as ph:
        xT = [ph.sb(f"xT{i}", [P, KC, P]) for i in range(2)]
        pG = [ph.ps(f"pG{i}") for i in range(2)]
        pU = [ph.ps(f"pU{i}") for i in range(2)]
        pT = [ph.ps(f"pT{i}") for i in range(2)]
        pO = [ph.ps(f"pO{i}") for i in range(2)]
        act_g = [ph.sb(f"act_g{i}", [P, chunk]) for i in range(2)]
        hid = [ph.sb(f"hid{i}", [P, chunk]) for i in range(2)]
        hidw = [ph.sb(f"hidw{i}", [P, chunk]) for i in range(2)]
        hT = [ph.sb(f"hT{i}", [P, KT, P]) for i in range(2)]
        (xT_ready, gu_ps, silu_done, hid_done, hidw_done, hT_ps, hT_ready, down_done, out_ps, added) = (
            ph.sem(n) for n in ("xT_ready", "gu_ps", "silu_done", "hid_done", "hidw_done", "hT_ps", "hT_ready",
                                "down_done", "out_ps", "added"))
        block = ph.block()

        def ring(eng, body):
            for c in range(NC):
                body(0, 0, c, c, c >= 2)
            for c in range(NC):
                body(1, 1, c, NC + c, True)
            with eng.Fori(1, B // 2) as i:
                for p in range(2):
                    for c in range(NC):
                        body(2 * i + p, p, c, (2 * i + p) * NC + c, True)

        @block.gpsimd
        def _(pool):
            def copy(b, p):
                pool.tensor_copy(xT[p][:], G["xnT"][:, :, bass.ds(b * P, P)]).then_inc(xT_ready, 1)

            copy(0, 0)
            copy(1, 1)

            def body(b, p, c, q, old):
                w = weights(b, c)
                if w is not None:
                    if old:
                        pool.wait_ge(hT_ps, q - 1)
                    hold(pool, hid_done, q + 1, G["spare"])
                    n = w.shape[1]
                    pool.tensor_tensor(hidw[c % 2][:].rearrange("p (e i) -> p e i", e=n),
                                       hid[c % 2][:].rearrange("p (e i) -> p e i", e=n),
                                       bc(w, chunk // n), ALU.mult).then_inc(hidw_done, 1)
                if c == NC - 1:
                    hold(pool, gu_ps, q + 1, G["spare"])
                    copy((b + 2) % B, p)

            ring(pool, body)

        @block.tensor
        def _(pe):
            for s in loaded:
                pe.wait_ge(*s)

            def up(b, p, c, q, old):
                if c == 0:
                    pe.wait_ge(xT_ready, b + 1)
                if old:
                    pe.wait_ge(hid_done, q - 1)
                for ps, w in ((pG[c % 2], w_gate), (pU[c % 2], w_up)):
                    for k in range(KC):
                        last = pe.matmul(ps[:, 0:chunk], lhsT=xT[p][:, k, :], rhs=w(k, c), start=(k == 0),
                                         stop=(k == KC - 1))
                last.then_inc(gu_ps, 1)

            def turn_hidden(b, c, q, old):
                if weights(b, c) is None:
                    pe.wait_ge(hid_done, q + 1)
                else:
                    pe.wait_ge(hidw_done, b * NW + sum(weighted[:c + 1]))
                if old:
                    pe.wait_ge(hT_ready, q - 1)
                for k in range(KT):
                    last = pe.transpose(pT[c % 2][:, k * P:(k + 1) * P], hidw[c % 2][:, k * P:(k + 1) * P],
                                        G["ident"][:])
                last.then_inc(hT_ps, 1)

            def down(b, p, c, q):
                pe.wait_ge(hT_ready, q + 1)
                if c == 0 and not (isinstance(b, int) and b < 2):
                    pe.wait_ge(added, b - 1)
                for k in range(KT):
                    last = pe.matmul(pO[p][:, 0:C], lhsT=hT[c % 2][:, k, :], rhs=w_down(c * KT + k),
                                     start=(c == 0 and k == 0), stop=(c == NC - 1 and k == KT - 1))
                last.then_inc(down_done, 1)

            def body(b, p, c, q, old):
                up(b, p, c, q, old)
                if old or c >= 1:
                    turn_hidden(b if c >= 1 else b - 1, (c - 1) % NC, q - 1, old and not (isinstance(q, int) and q < 3))
                if old or c >= 2:
                    down(b if c >= 2 else b - 1, p if c >= 2 else 1 - p, (c - 2) % NC, q - 2)

            ring(pe, body)
            Q = B * NC
            turn_hidden(B - 1, NC - 1, Q - 1, True)
            down(B - 1, 1, NC - 2, Q - 2)
            down(B - 1, 1, NC - 1, Q - 1)

        @block.scalar
        def _(act):
            def body(b, p, c, q, old):
                act.wait_ge(gu_ps, q + 1)
                if old:
                    act.wait_ge(hid_done, q - 1)
                act.activation(act_g[c % 2][:], pG[c % 2][:, 0:chunk], ACT.Silu).then_inc(silu_done, 1)
                if old or c >= 1:
                    evacuate((c - 1) % NC, q - 1, old and not (isinstance(q, int) and q < 3))

            def evacuate(c, q, old):
                act.wait_ge(hT_ps, q + 1)
                if old:
                    act.wait_ge(down_done, q - 1)
                act.activation(hT[c % 2][:].rearrange("p k t -> p (k t)"), pT[c % 2][:, 0:chunk],
                               ACT.Copy).then_inc(hT_ready, 1)

            ring(act, body)
            evacuate(NC - 1, B * NC - 1, True)

        @block.vector
        def _(dve):
            def finish(b, p):
                dve.wait_ge(down_done, b * NC + NC)
                x = G["x_all"][:, b, :]
                dve.scalar_tensor_tensor(x, pO[p][:, 0:C], G["tg"][:, gate:gate + 1], x,
                                         ALU.mult, ALU.add).then_inc(added, 1)

            def body(b, p, c, q, old):
                w = weights(b, c)
                dve.wait_ge(silu_done, q + 1)
                if old:
                    dve.wait_ge(hT_ps, q - 1)
                if w is not None:
                    dve.tensor_tensor(hid[c % 2][:], act_g[c % 2][:], pU[c % 2][:, 0:chunk],
                                      ALU.mult).then_inc(hid_done, 1)
                else:
                    dve.tensor_tensor(hidw[c % 2][:], act_g[c % 2][:], pU[c % 2][:, 0:chunk],
                                      ALU.mult).then_inc(hid_done, 1)
                if c == min(3, NC - 1) and not (isinstance(b, int) and b == 0):
                    finish(b - 1, 1 - p)

            ring(dve, body)
            finish(B - 1, 1)


def phase_gating0(nc, D, G):
    NE, TOPK = 32, 8
    CAP = 2 * (B * P * TOPK // NE)
    with Phase(nc, "gate0") as ph:
        pT, pL, pR = ph.ps("pT"), ph.ps("pL"), ph.ps("pR")
        nm = Norm(ph, G, pT)
        probs, replaced = ph.sb("probs", [P, B, NE]), ph.sb("replaced", [P, B, NE])
        mask, maskb = ph.sb("mask", [P, B, NE]), ph.sb("maskb", [P, B, NE], BF16)
        before, beforeb = ph.sb("before", [P, B, NE]), ph.sb("beforeb", [P, B, NE], BF16)
        top = ph.sb("top", [P, B, 8])
        red, rec = ph.sb("red", [P, B]), ph.sb("rec", [P, B])
        lower = ph.sb("lower", [P, P], BF16)
        onesb = ph.sb("onesb", [P, P], BF16)
        const_in, logits, steps, exp_done, masks, ranks = (
            ph.sem(n) for n in ("const_in", "logits", "steps", "exp_done", "masks", "ranks"))
        block = ph.block()
        gw, w_all = G["l0_gate_w"], G["w_all"]

        @block.gpsimd
        def _(pool):
            sweep(pool, lambda b, p: nm.pool(pool, b, p), lambda b, p: None)

        @block.sync
        def _(sp):
            sp.dma_start(lower[:].bitcast(U16), D["c_lower"]).then_inc(const_in, 16)
            sp.dma_start(onesb[:].bitcast(U16), D["c_onesb"]).then_inc(const_in, 16)

        @block.tensor
        def _(pe):
            pe.wait_ge(*G["loaded"]["small"])
            pe.wait_ge(const_in, 32)

            def turn(b, p):
                pe.wait_ge(nm.xT_ready, b + 1)
                for k in range(KC):
                    last = pe.matmul(pL[:, bass.ds(b * NE, NE)], lhsT=nm.xT[p][:, k, :], rhs=gw[:, k, :],
                                     start=(k == 0), stop=(k == KC - 1))
                last.then_inc(logits, 1)

            sweep(pe, lambda b, p: nm.tensor(pe, b, p), turn)
            pe.wait_ge(masks, 1)
            pe.matmul(pR[:], lhsT=lower[:], rhs=maskb[:].rearrange("p b e -> p (b e)"), start=True, stop=False)
            pe.matmul(pR[:], lhsT=onesb[:], rhs=beforeb[:].rearrange("p b e -> p (b e)"), start=False,
                      stop=True).then_inc(ranks, 1)

        @block.scalar
        def _(act):
            def front(b, p):
                act.wait_ge(nm.xT_ps, b + 1)
                act.activation(G["xnT"][:, :, bass.ds(b * P, P)], pT[:, 0:C].rearrange("p (k t) -> p k t", k=KC),
                               ACT.Copy)
                nm.scalar(act, b, p)

            front(0, 0)
            front(1, 1)
            with act.Fori(1, B // 2) as i:
                act.wait_ge(logits, 2 * i - 1)
                front(2 * i, 0)
                act.wait_ge(logits, 2 * i)
                front(2 * i + 1, 1)
            act.wait_ge(steps, 2)
            act.activation(probs[:], probs[:], ACT.Exp).then_inc(exp_done, 1)

        @block.vector
        def _(dve):
            sweep(dve, lambda b, p: nm.front(dve, b, p), lambda b, p: None)
            ch = Chain(dve, steps, 14 + 2 * B + (B - 1))
            ch.turn(0)
            dve.wait_ge(logits, B)
            L = pL[:].rearrange("p (b e) -> p b e", e=NE)
            ch(dve.tensor_reduce(red[:], L, AX.X, ALU.max))
            ch(dve.tensor_tensor(probs[:], L, bc(red[:], NE), ALU.subtract))
            dve.wait_ge(exp_done, 1)
            ch(dve.tensor_reduce(red[:], probs[:], AX.X, ALU.add))
            ch(dve.reciprocal(rec[:], red[:]))
            ch(dve.tensor_tensor(probs[:], probs[:], bc(rec[:], NE), ALU.mult))
            for b in range(B):
                ch(dve.max(top[:, b, :], probs[:, b, :]))
                ch(dve.match_replace(replaced[:, b, :], top[:, b, :], probs[:, b, :], -1.0))
            ch(dve.tensor_scalar(mask[:], replaced[:], 0.0, None, ALU.is_lt))
            ch(dve.tensor_copy(maskb[:], mask[:]))
            ch(dve.memset(before[:, 0, :], 0.0))
            for b in range(1, B):
                ch(dve.tensor_tensor(before[:, b, :], before[:, b - 1, :], mask[:, b - 1, :], ALU.add))
            ch(dve.tensor_copy(beforeb[:], before[:]))
            dve.sem_inc(masks, 1)
            ch(dve.tensor_tensor(probs[:], probs[:], mask[:], ALU.mult))
            ch(dve.tensor_reduce(red[:], probs[:], AX.X, ALU.add))
            ch(dve.reciprocal(rec[:], red[:]))
            ch(dve.tensor_tensor(probs[:], probs[:], bc(rec[:], NE), ALU.mult))
            dve.wait_ge(const_in, 32)
            dve.wait_ge(ranks, 1)
            ch(dve.tensor_scalar(mask[:], pR[:].rearrange("p (b e) -> p b e", e=NE), float(CAP), None, ALU.is_lt))
            dve.tensor_tensor(w_all[:], probs[:], mask[:], ALU.mult)



class Turned:

    def __init__(self, ph, G, ps_q, ps_k, k_tiles=4):
        self.G, self.ps_q, self.ps_k, self.kt = G, ps_q, ps_k, k_tiles
        self.rows_ready, self.turned_ps, self.ready = (ph.sem(n) for n in ("rows_ready", "turned_ps", "qk_ready"))
        self.q = ph.sb("q_rows", [P, NH, SLOT])
        self.k = ph.sb("k_rows", [P, 4 * k_tiles, SLOT])
        self.qT = [ph.sb(f"qT{i}", [P, 4, P]) for i in range(2)]
        self.kT = [ph.sb(f"kT{i}", [P, k_tiles, P]) for i in range(2)]

    def clear(self, dve):
        dve.memset(self.q[:], 0.0)
        dve.memset(self.k[:], 0.0).then_inc(self.rows_ready, 1)
        dve.wait_ge(self.rows_ready, 1)

    def tensor(self, pe, b):
        pe.wait_ge(self.rows_ready, b + 2)
        after(pe, self.ready, b)
        for m in range(4):
            pe.transpose(self.ps_q[:, m * P:(m + 1) * P], self.q[:, 4 * m:4 * m + 4, :].rearrange("p h d -> p (h d)"),
                         self.G["ident"][:])
        for m in range(self.kt):
            last = pe.transpose(self.ps_k[:, m * P:(m + 1) * P],
                                self.k[:, 4 * m:4 * m + 4, :].rearrange("p h d -> p (h d)"), self.G["ident"][:])
        last.then_inc(self.turned_ps, 1)

    def scalar(self, act, b, p):
        act.wait_ge(self.turned_ps, b + 1)
        act.activation(self.kT[p][:].rearrange("p m t -> p (m t)"), self.ps_k[:, 0:self.kt * P], ACT.Copy)
        act.activation(self.qT[p][:].rearrange("p m t -> p (m t)"), self.ps_q[:], ACT.Copy).then_inc(self.ready, 1)


def project(pe, out, xT, w, cols=slice(None)):
    for k in range(KC):
        last = pe.matmul(out, lhsT=xT[:, k, :], rhs=w[:, k, cols], start=(k == 0), stop=(k == KC - 1))
    return last


def phase_l1_attention(nc, D, G):
    W = G["W"]
    with Phase(nc, "l1x") as ph:
        pT, pQK, pV, pTq, pTk = (ph.ps(n) for n in ("pT", "pQK", "pV", "pTq", "pTk"))
        pS = [ph.ps("pS0"), ph.ps("pS1")]
        pO = ph.ps("pO")
        nm = Norm(ph, G, pT)
        tq = Turned(ph, G, pTq, pTk)
        cT = [ph.sb(f"cT{i}", [P, KC, P]) for i in range(2)]
        v = [ph.sb(f"v{i}", [P, NH, HD + 1]) for i in range(2)]
        sc = [ph.sb(f"sc{i}", [P, 4 * P]) for i in range(2)]
        ex = [ph.sb(f"ex{i}", [P, 4, P]) for i in range(2)]
        den, rec = ph.sb("den", [P, NH]), ph.sb("rec", [P, NH])
        att = ph.sb("att", [P, C])
        attT = ph.sb("attT", [P, KC, P])
        delta = ph.sb("delta", [P, C])
        zed = [ph.sb(f"zed{i}", [P, C]) for i in range(2)]
        stats, mv, rstd = ph.sb("stats", [P, 6]), ph.sb("mv", [P, 2]), ph.sb("rstd", [P, 1])
        bq, bo, gam, bet = (ph.sb(n, [P, C]) for n in ("bq", "bo", "gam", "bet"))
        rs = ph.sb("rs", [P, 1])
        mask_i = ph.sb("mask_i", [P, B], I32)
        upper = ph.sb("upper", [P, B])
        (mask_in, consts, cT_ready, qkv_ps, v_ready, sc_ps, clipped, exp_done, pv_done, den_steps, att_ready,
         attT_ps, attT_ready, out_ps, tail_steps, stats2, rstd2, zed_ready, tail_pool) = (
            ph.sem(n) for n in ("mask_in", "consts", "cT_ready", "qkv_ps", "v_ready", "sc_ps", "clipped", "exp_done",
                                "pv_done", "den_steps", "att_ready", "attT_ps", "attT_ready", "out_ps", "tail_steps",
                                "stats2", "rstd2", "zed_ready", "tail_pool"))
        block = ph.block()

        @block.sync
        def _(sp):
            sp.dma_start(mask_i[:], D["mask_T"]).then_inc(mask_in, 16)
            G["load"](sp, "l2")
            G["load"](sp, "l2f")

        @block.gpsimd
        def _(pool):
            def front(b, p):
                nm.pool(pool, b, p)
                if not (isinstance(b, int) and b < 2):
                    hold(pool, qkv_ps, b - 1, G["spare"])
                pool.tensor_copy(cT[p][:], G["ctxT"][:, :, bass.ds(b * P, P)]).then_inc(cT_ready, 1)

            def body(b, p):
                pool.wait_ge(stats2, b + 1)
                pool.tensor_tensor(rstd[:], mv[:, 1:2], G["eps"][:, 0:1], ALU.add).then_inc(rstd2, 1)
                pool.wait_ge(rstd2, 2 * b + 1)
                pool.tensor_tensor(rstd[:], rstd[:], G["minus_half"][:, 0:1], ALU.pow).then_inc(rstd2, 1)
                pool.wait_ge(zed_ready, b + 1)
                pool.tensor_tensor(zed[p][:], zed[p][:], gam[:], ALU.mult).then_inc(tail_pool, 1)
                pool.wait_ge(tail_pool, 3 * b + 1)
                pool.tensor_tensor(zed[p][:], zed[p][:], bet[:], ALU.add).then_inc(tail_pool, 1)
                hold(pool, tail_pool, 3 * b + 2, G["spare"])
                x = G["x_all"][:, b, :]
                pool.tensor_tensor(x, zed[p][:], x, ALU.add).then_inc(tail_pool, 1)

            sweep(pool, front, body)

        @block.tensor
        def _(pe):
            pe.wait_ge(*G["loaded"]["small"])

            def front(b, p):
                nm.tensor(pe, b, p)
                pe.wait_ge(nm.xT_ready, b + 1)
                pe.wait_ge(cT_ready, b + 1)
                after(pe, v_ready, b)
                project(pe, pQK[:, 0:C], nm.xT[p], W["L1_xattn_Wq"])
                project(pe, pQK[:, C:2 * C], cT[p], W["L1_xattn_Wk"])
                project(pe, pV[:, 0:C], cT[p], W["L1_xattn_Wv"]).then_inc(qkv_ps, 1)
                tq.tensor(pe, b)

            def scores(b, p, s):
                if s >= 2:
                    pe.wait_ge(clipped, 4 * b + s - 1)
                for m in range(4):
                    rows = slice(SLOT * s, SLOT * s + HD)
                    last = pe.matmul(pS[s % 2][:, m * P:(m + 1) * P], lhsT=tq.kT[p][rows, m, :],
                                     rhs=tq.qT[p][rows, m, :], start=True, stop=True)
                last.then_inc(sc_ps, 1)

            def values(b, p, s):
                pe.wait_ge(exp_done, 4 * b + s + 1)
                for m in range(4):
                    h = 4 * m + s
                    last = pe.matmul(pO[:, h * (HD + 1):(h + 1) * (HD + 1)], lhsT=ex[s % 2][:, m, :],
                                     rhs=v[p][:, h, :], start=True, stop=True)
                last.then_inc(pv_done, 1)

            def body(b, p):
                pe.wait_ge(tq.ready, b + 1)
                scores(b, p, 0)
                scores(b, p, 1)
                values(b, p, 0)
                scores(b, p, 2)
                values(b, p, 1)
                scores(b, p, 3)
                values(b, p, 2)
                values(b, p, 3)
                pe.wait_ge(att_ready, b + 1)
                for k in range(KC):
                    last = pe.transpose(pT[:, C + k * P:C + (k + 1) * P], att[:, k * P:(k + 1) * P], G["ident"][:])
                last.then_inc(attT_ps, 1)
                pe.wait_ge(attT_ready, b + 1)
                project(pe, pV[:, C:2 * C], attT, W["L1_xattn_Wo"]).then_inc(out_ps, 1)

            sweep(pe, front, body)

        @block.scalar
        def _(act):
            def front(b, p):
                nm.scalar(act, b, p)
                tq.scalar(act, b, p)

            def body(b, p):
                for s in range(4):
                    act.wait_ge(clipped, 4 * b + s + 1)
                    if s >= 2:
                        act.wait_ge(pv_done, 4 * b + s - 1)
                    act.activation(ex[s % 2][:].rearrange("p m t -> p (m t)"), sc[s % 2][:],
                                   ACT.Exp).then_inc(exp_done, 1)
                act.wait_ge(attT_ps, b + 1)
                act.activation(attT[:].rearrange("p k t -> p (k t)"), pT[:, C:2 * C],
                               ACT.Copy).then_inc(attT_ready, 1)

            sweep(act, front, body)

        @block.vector
        def _(dve):
            dve.wait_ge(*G["loaded"]["small"])
            dve.wait_ge(mask_in, 16)
            tq.clear(dve)
            ch = Chain(dve, consts, 6)
            ch.turn(0)
            ch(dve.tensor_copy(upper[:], mask_i[:]))
            ch(dve.tensor_scalar(upper[:], upper[:], 0.5, 100.0, ALU.is_gt, ALU.mult))
            ch(dve.tensor_scalar(upper[:], upper[:], -50.0, None, ALU.add))
            ch(dve.tensor_scalar(rs[:], W["L1_xattn_residual_scale"][:, 0, :], 0.0, 0.3, ALU.max, ALU.min))
            ch(dve.tensor_scalar(bo[:], W["L1_xattn_bo"][:, 0, :], rs[:, 0:1], None, ALU.mult))
            dve.memset(v[0][:], 1.0)
            dve.memset(v[1][:], 1.0)
            dve.tensor_scalar(bq[:], W["L1_xattn_bq"][:, 0, :], 0.25, None, ALU.mult)
            dve.tensor_scalar(gam[:], W["L1_xattn_ln_gamma"][:, 0, :], G["tg"][:, 1:2], None, ALU.mult)
            ch(dve.tensor_scalar(bet[:], W["L1_xattn_ln_beta"][:, 0, :], G["tg"][:, 1:2], None, ALU.mult))

            def front(b, p):
                nm.front(dve, b, p)
                dve.wait_ge(qkv_ps, b + 1)
                after(dve, tq.turned_ps, b)
                dve.scalar_tensor_tensor(tq.q[:, :, 0:HD], heads(pQK[:, 0:C]), 0.25, heads(bq[:]), ALU.mult, ALU.add)
                dve.tensor_tensor(tq.k[:, :, 0:HD], heads(pQK[:, C:2 * C]), heads(W["L1_xattn_bk"][:, 0, :]),
                                  ALU.add).then_inc(tq.rows_ready, 1)
                if not (isinstance(b, int) and b < 2):
                    dve.wait_ge(pv_done, 4 * (b - 1))
                dve.tensor_tensor(v[p][:, :, 0:HD], heads(pV[:, 0:C]), heads(W["L1_xattn_bv"][:, 0, :]),
                                  ALU.add).then_inc(v_ready, 1)

            def body(b, p):
                for s in range(4):
                    dve.wait_ge(sc_ps, 4 * b + s + 1)
                    if s >= 2:
                        dve.wait_ge(exp_done, 4 * b + s - 1)
                    dve.tensor_scalar(sc[s % 2][:], pS[s % 2][:], -50.0, upper[:, b:b + 1] if isinstance(b, int)
                                      else upper[:, bass.ds(b, 1)], ALU.max, ALU.min).then_inc(clipped, 1)
                o = pO[:, 0:NH * (HD + 1)].rearrange("p (h d) -> p h d", h=NH)
                dve.wait_ge(pv_done, 4 * b + 4)
                dve.tensor_scalar(den[:], o[:, :, HD:HD + 1].rearrange("p h d -> p (h d)"), 1.0 + 1e-8, None,
                                  ALU.mult).then_inc(den_steps, 1)
                dve.wait_ge(den_steps, 2 * b + 1)
                dve.reciprocal(rec[:], den[:]).then_inc(den_steps, 1)
                dve.wait_ge(den_steps, 2 * b + 2)
                dve.tensor_tensor(heads(att[:]), o[:, :, 0:HD], bc(rec[:], HD), ALU.mult).then_inc(att_ready, 1)
                dve.wait_ge(out_ps, b + 1)
                dve.scalar_tensor_tensor(delta[:], pV[:, C:2 * C], rs[:, 0:1], bo[:], ALU.mult,
                                         ALU.add).then_inc(tail_steps, 1)
                dve.wait_ge(tail_steps, 2 * b + 1)
                dve.bn_stats(stats[:], delta[:]).then_inc(tail_steps, 1)
                hold(dve, tail_steps, 2 * b + 2, G["spare"])
                dve.bn_aggr(mv[:], stats[:]).then_inc(stats2, 1)
                dve.wait_ge(rstd2, 2 * b + 2)
                if not (isinstance(b, int) and b < 2):
                    dve.wait_ge(tail_pool, 3 * (b - 1))
                dve.tensor_scalar(zed[p][:], delta[:], mv[:, 0:1], rstd[:, 0:1], ALU.subtract,
                                  ALU.mult).then_inc(zed_ready, 1)

            sweep(dve, front, body)


class HeadSoftmax:

    def __init__(self, ph, G, tq, pS, pP, pO, mask_id, mask_of, v_of, k_of):
        self.G, self.tq, self.pS, self.pP, self.pO = G, tq, pS, pP, pO
        self.mask_id, self.mask_of, self.v_of, self.k_of = mask_id, mask_of, v_of, k_of
        self.sc_ps, self.max_ready, self.exp_done, self.pT_ps, self.pT_ready, self.pv_done, self.norm_steps = (
            ph.sem(n) for n in ("sc_ps", "max_ready", "exp_done", "pT_ps", "pT_ready", "pv_done", "norm_steps"))
        self.negmax = [ph.sb(f"negmax{i}", [P, 4]) for i in range(2)]
        self.ex = [ph.sb(f"ex{i}", [P, 4, P]) for i in range(2)]
        self.exT = [ph.sb(f"exT{i}", [P, 4, P]) for i in range(2)]
        self.sums = ph.sb("sums", [P, 4, 4])
        self.rec = ph.sb("rec", [P, NH])

    def scores(self, pe, b, p, s):
        after(pe, self.exp_done, 4 * b + s - 1)
        bank = self.pS[s % 2]
        pe.matmul(bank[:], lhsT=self.mask_id[:], rhs=self.mask_of(p), start=True, stop=True)
        rows = slice(SLOT * s, SLOT * s + HD)
        for m in range(4):
            last = pe.matmul(bank[:, m * P:(m + 1) * P], lhsT=self.tq.qT[p][rows, m, :],
                             rhs=self.k_of(p, m)[rows, :], start=False, stop=True, skip_group_check=True)
        last.then_inc(self.sc_ps, 1)

    def turn(self, pe, b, p, s):
        pe.wait_ge(self.exp_done, 4 * b + s + 1)
        after(pe, self.pT_ready, 4 * b + s)
        for m in range(4):
            last = pe.transpose(self.pP[:, m * P:(m + 1) * P], self.ex[s % 2][:, m, :], self.G["ident"][:])
        last.then_inc(self.pT_ps, 1)

    def values(self, pe, b, p, s):
        pe.wait_ge(self.pT_ready, 4 * b + s + 1)
        for m in range(4):
            h = 4 * m + s
            last = pe.matmul(self.pO[:, h * HD:(h + 1) * HD], lhsT=self.exT[s % 2][:, m, :], rhs=self.v_of(p, h),
                             start=True, stop=True)
        last.then_inc(self.pv_done, 1)

    def tensor(self, pe, b, p):
        pe.wait_ge(self.tq.ready, b + 1)
        self.scores(pe, b, p, 0)
        self.scores(pe, b, p, 1)
        self.turn(pe, b, p, 0)
        self.scores(pe, b, p, 2)
        self.turn(pe, b, p, 1)
        self.values(pe, b, p, 0)
        self.scores(pe, b, p, 3)
        self.turn(pe, b, p, 2)
        self.values(pe, b, p, 1)
        self.turn(pe, b, p, 3)
        self.values(pe, b, p, 2)
        self.values(pe, b, p, 3)

    def scalar(self, act, b, p):
        for s in range(4):
            act.wait_ge(self.max_ready, 4 * b + s + 1)
            after(act, self.pT_ps, 4 * b + s - 1)
            for m in range(4):
                ins = act.activation(self.ex[s % 2][:, m, :], self.pS[s % 2][:, m * P:(m + 1) * P], ACT.Exp,
                                     bias=self.negmax[s % 2][:, m:m + 1], accum_out=self.sums[:, m, s:s + 1])
            ins.then_inc(self.exp_done, 1)

    def vector(self, dve, b, p):
        def evacuate(s):
            dve.wait_ge(self.pT_ps, 4 * b + s + 1)
            after(dve, self.pv_done, 4 * b + s - 1)
            dve.tensor_copy(self.exT[s % 2][:].rearrange("p m t -> p (m t)"), self.pP[:]).then_inc(self.pT_ready, 1)

        for s in range(4):
            dve.wait_ge(self.sc_ps, 4 * b + s + 1)
            after(dve, self.exp_done, 4 * b + s - 1)
            dve.tensor_reduce(self.negmax[s % 2][:], self.pS[s % 2][:].rearrange("p (m t) -> p m t", m=4), AX.X,
                              ALU.max, negate=True).then_inc(self.max_ready, 1)
            if s >= 1:
                evacuate(s - 1)
        evacuate(3)

    def normalise(self, dve, out, b, signal):
        dve.wait_ge(self.exp_done, 4 * b + 4)
        dve.reciprocal(self.rec[:], self.sums[:].rearrange("p m s -> p (m s)")).then_inc(self.norm_steps, 1)
        dve.wait_ge(self.pv_done, 4 * b + 4)
        dve.wait_ge(self.norm_steps, b + 1)
        dve.tensor_tensor(heads(out), heads(self.pO[:, 0:C] if self.pO_cols is None else self.pO_cols),
                          bc(self.rec[:], HD), ALU.mult).then_inc(signal, 1)

    pO_cols = None


def phase_l1_ffn(nc, D, G):
    W = G["W"]
    with Phase(nc, "l1f") as ph:
        pT, pQK, pV, pTq = (ph.ps(n) for n in ("pT", "pQK", "pV", "pTq"))
        pS = [ph.ps("pS0"), ph.ps("pS1")]
        pP, pO = ph.ps("pP"), ph.ps("pO")
        nm = Norm(ph, G, pT)
        tq = Turned(ph, G, pTq, pO[:, C:2 * C], k_tiles=1)
        causal = ph.sb("causal", [P, 4, P], BF16)
        vs = [ph.sb(f"vs{i}", [P, HD]) for i in range(2)]
        picked = ph.sb("picked", [P, NH, HD])
        shared = ph.sb("shared", [P, HD])
        count = ph.sb("count", [P, NH])
        g, hit, val = ph.sb("g", [P, NH]), ph.sb("hit", [P, NH]), ph.sb("val", [P, NH])
        one, total = ph.sb("one", [P, 1]), ph.sb("total", [P, 1])
        att = ph.sb("att", [P, C])
        const_in, qkv_ps, gate_neg, gate_exp, steps, qkv_read, att_ready, added = (
            ph.sem(n) for n in ("const_in", "qkv_ps", "gate_neg", "gate_exp", "steps", "qkv_read", "att_ready",
                                "added"))
        sm = HeadSoftmax(ph, G, tq, pS, pP, pO, G["identb"], lambda p: causal[:].rearrange("p m t -> p (m t)"),
                         lambda p, h: vs[p][:], lambda p, m: tq.kT[p][:, 0, :])
        block = ph.block()

        @block.sync
        def _(sp):
            sp.dma_start(causal[:].bitcast(U16), D["c_causal"]).then_inc(const_in, 16)
            sp.dma_start(count[:], D["c_count"].partition_broadcast(P)).then_inc(const_in, 16)

        @block.gpsimd
        def _(pool):
            sweep(pool, lambda b, p: nm.pool(pool, b, p), lambda b, p: None)

        @block.tensor
        def _(pe):
            pe.wait_ge(*G["loaded"]["small"])
            pe.wait_ge(const_in, 32)

            def front(b, p):
                nm.tensor(pe, b, p)
                pe.wait_ge(nm.xT_ready, b + 1)
                after(pe, qkv_read, b)
                project(pe, pV[:, 0:C + NH], nm.xT[p], W["W_vg"])
                project(pe, pQK[:], nm.xT[p], W["W_qk"]).then_inc(qkv_ps, 1)
                tq.tensor(pe, b)

            sweep(pe, front, lambda b, p: sm.tensor(pe, b, p))

        @block.scalar
        def _(act):
            def front(b, p):
                nm.scalar(act, b, p)
                act.wait_ge(gate_neg, b + 1)
                act.activation(g[:], pV[:, C:C + NH], ACT.Exp, bias=one[:, 0:1],
                               accum_out=total[:, 0:1]).then_inc(gate_exp, 1)
                tq.scalar(act, b, p)

            sweep(act, front, lambda b, p: sm.scalar(act, b, p))

        @block.vector
        def _(dve):
            dve.wait_ge(const_in, 32)
            tq.clear(dve)
            ch = Chain(dve, steps, 11)

            def front(b, p):
                nm.front(dve, b, p)
                ch.turn(b)
                dve.wait_ge(qkv_ps, b + 1)
                dve.tensor_reduce(one[:], pV[:, C:C + NH], AX.X, ALU.max, negate=True).then_inc(gate_neg, 1)
                dve.wait_ge(gate_exp, b + 1)
                ch(dve.tensor_reduce(val[:, 0:1], g[:], AX.X, ALU.max))
                ch(dve.tensor_scalar(hit[:], g[:], val[:, 0:1], None, ALU.is_ge))
                ch(dve.tensor_tensor(hit[:], hit[:], count[:], ALU.mult))
                ch(dve.tensor_reduce(val[:, 0:1], hit[:], AX.X, ALU.min))
                ch(dve.tensor_scalar(hit[:], count[:], val[:, 0:1], None, ALU.is_equal))
                ch(dve.reciprocal(total[:], total[:]))
                ch(dve.tensor_scalar(val[:], hit[:], total[:, 0:1], None, ALU.mult))
                ch(dve.tensor_tensor(picked[:], heads(pQK[:, C:2 * C]), bc(hit[:], HD), ALU.mult))
                ch(dve.tensor_reduce(shared[:], picked[:].rearrange("p h d -> p d h"), AX.X, ALU.add))
                ch(dve.tensor_tensor(picked[:], heads(pV[:, 0:C]), bc(val[:], HD), ALU.mult))
                if not (isinstance(b, int) and b < 2):
                    dve.wait_ge(sm.pv_done, 4 * (b - 1))
                ch(dve.tensor_reduce(vs[p][:], picked[:].rearrange("p h d -> p d h"), AX.X, ALU.add))
                after(dve, tq.turned_ps, b)
                dve.tensor_scalar(tq.q[:, :, 0:HD], heads(pQK[:, 0:C]), 0.25, None, ALU.mult).then_inc(qkv_read, 1)
                dve.tensor_copy(tq.k[:, :, 0:HD], shared[:].unsqueeze(1).to_broadcast([P, 4, HD])
                                ).then_inc(tq.rows_ready, 1)

            def body(b, p):
                sm.vector(dve, b, p)
                sm.normalise(dve, att[:], b, att_ready)
                dve.wait_ge(att_ready, b + 1)
                x = G["x_all"][:, b, :]
                dve.scalar_tensor_tensor(x, att[:], G["tg"][:, 5:6], x, ALU.mult, ALU.add).then_inc(added, 1)

            sweep(dve, front, body)


def phase_l3_attention(nc, D, G):
    W = G["W"]
    with Phase(nc, "l3x") as ph:
        pT, pQK, pV, pTq, pTk = (ph.ps(n) for n in ("pT", "pQK", "pV", "pTq", "pTk"))
        pS = [ph.ps("pS0"), ph.ps("pS1")]
        pP = ph.ps("pP")
        nm = Norm(ph, G, None)
        tq = Turned(ph, G, pTq, pTk)
        cT = [ph.sb(f"cT{i}", [P, KC, P]) for i in range(2)]
        v = [ph.sb(f"v{i}", [P, C]) for i in range(2)]
        mask = [ph.sb(f"mask{i}", [P, P]) for i in range(2)]
        qwT = {n: ph.sb(f"w{n}T", [P, KC, C], BF16) for n in "qo"}
        sw = {n: ph.sb(f"sw{n}", [P, C]) for n in "qo"}
        bias = {n: ph.sb(f"b{n}", [P, C]) for n in "qo"}
        wamax, winv, wrows, wq8 = ph.sb("wamax", [P, 2]), ph.sb("winv", [P, 2]), ph.sb("wrows", [P, KC, C]), ph.sb(
            "wq8", [P, KC, C], BF16)
        scale_cols = ph.sb("scale_cols", [P, P])
        qx = Quant(ph, G, "qx", C, 1e-8)
        qa = Quant(ph, G, "qa", C, 1e-8)
        xqT = ph.sb("xqT", [P, KC, P], BF16)
        aqT = ph.sb("aqT", [P, KC, P], BF16)
        qpre = ph.sb("qpre", [P, C])
        att, outp = ph.sb("att", [P, C]), ph.sb("outp", [P, C])
        pTb = pT[:, 0:C].bitcast(BF16)
        (wsteps, w_ps, w_read, cT_ready, xq_ps, xqT_ready, kv_read, qkv_ps, q_steps, att_ready, aq_ps, aqT_ready,
         out_ps, out_steps, added) = (
            ph.sem(n) for n in ("wsteps", "w_ps", "w_read", "cT_ready", "xq_ps", "xqT_ready", "kv_read", "qkv_ps",
                                "q_steps", "att_ready", "aq_ps", "aqT_ready", "out_ps", "out_steps", "added"))
        mask_in = [ph.sem(f"mask_in{i}") for i in range(2)]
        sm = HeadSoftmax(ph, G, tq, pS, pP, None, G["ident"],
                         lambda p: mask[p][:].unsqueeze(1).to_broadcast([P, 4, P]),
                         lambda p, h: v[p][:, h * HD:(h + 1) * HD], lambda p, m: tq.kT[p][:, m, :])
        sm.pO = pV[:, C:2 * C]
        sm.pO_cols = sm.pO
        block = ph.block()

        @block.sync
        def _(sp):
            for p in range(2):
                sp.dma_start(mask[p][:], D["mask_BxSxS2_ff0"][p]).then_inc(mask_in[p], 16)
            with sp.Fori(0, B // 2 - 1) as i:
                for p in range(2):
                    sp.wait_ge(sm.sc_ps, 4 * (2 * i + p + 1))
                    sp.dma_start(mask[p][:], D["mask_BxSxS2_ff0"][2 * i + 2 + p]).then_inc(mask_in[p], 16)

        @block.gpsimd
        def _(pool):
            def front(b, p):
                nm.pool(pool, b, p)
                if not (isinstance(b, int) and b < 2):
                    hold(pool, qkv_ps, b - 1, G["spare"])
                pool.tensor_copy(cT[p][:], G["ctxT"][:, :, bass.ds(b * P, P)]).then_inc(cT_ready, 1)

            sweep(pool, front, lambda b, p: None)

        @block.tensor
        def _(pe):
            for j, n in enumerate("qo"):
                pe.wait_ge(wsteps, 12 * j + 10)
                for ko in range(KC):
                    for ki in range(KC):
                        last = pe.transpose(pTb[:, (2 * ko + ki) * P:(2 * ko + ki + 1) * P],
                                            wq8[:, ko, ki * P:(ki + 1) * P], G["identb"][:])
                last.then_inc(w_ps, 1)
                for ko in range(KC):
                    pe.wait_ge(wsteps, 12 * j + 11 + ko)
                    pe.matmul(pQK[:, ko * P:(ko + 1) * P], lhsT=scale_cols[:], rhs=G["ident"][:], start=True,
                              stop=True).then_inc(w_ps, 1)
                pe.wait_ge(w_read, 2 * j + 2)

            def front(b, p):
                pe.wait_ge(qx.ready, b + 1)
                after(pe, xqT_ready, b)
                for k in range(KC):
                    last = pe.transpose(pTb[:, k * P:(k + 1) * P], qx.q[:, k * P:(k + 1) * P], G["identb"][:])
                last.then_inc(xq_ps, 1)
                pe.wait_ge(cT_ready, b + 1)
                after(pe, kv_read, b)
                project(pe, pQK[:, C:2 * C], cT[p], W["L3_wk"])
                project(pe, pV[:, 0:C], cT[p], W["L3_wv"])
                pe.wait_ge(xqT_ready, b + 1)
                project(pe, pQK[:, 0:C], xqT, qwT["q"]).then_inc(qkv_ps, 1)
                tq.tensor(pe, b)

            def body(b, p):
                pe.wait_ge(mask_in[p], 8 * (b - p) + 16)
                sm.tensor(pe, b, p)
                pe.wait_ge(qa.ready, b + 1)
                for k in range(KC):
                    last = pe.transpose(pTb[:, C + k * P:C + (k + 1) * P], qa.q[:, k * P:(k + 1) * P], G["identb"][:])
                last.then_inc(aq_ps, 1)
                pe.wait_ge(aqT_ready, b + 1)
                project(pe, pT[:, C:2 * C], aqT, qwT["o"]).then_inc(out_ps, 1)

            sweep(pe, front, body)

        @block.scalar
        def _(act):
            def front(b, p):
                act.wait_ge(xq_ps, b + 1)
                act.activation(xqT[:].rearrange("p k t -> p (k t)"), pTb[:, 0:C], ACT.Copy).then_inc(xqT_ready, 1)
                tq.scalar(act, b, p)

            def body(b, p):
                sm.scalar(act, b, p)
                act.wait_ge(aq_ps, b + 1)
                act.activation(aqT[:].rearrange("p k t -> p (k t)"), pTb[:, C:2 * C], ACT.Copy).then_inc(aqT_ready, 1)

            sweep(act, front, body)

        @block.vector
        def _(dve):
            dve.wait_ge(*G["loaded"]["small"])
            tq.clear(dve)
            ch = Chain(dve, wsteps, 12)
            for j, n in enumerate("qo"):
                w = W[f"L3_w{n}"]
                ch.turn(j)
                ch(dve.tensor_reduce(wamax[:], w, AX.X, ALU.max, apply_absolute_value=True))
                ch(dve.tensor_scalar(wamax[:], wamax[:], 1.0 / 127.0, 1e-8, ALU.mult, ALU.max))
                ch(dve.reciprocal(winv[:], wamax[:]))
                for k in range(KC):
                    ch(dve.tensor_scalar(wrows[:, k, :], w[:, k, :], winv[:, k:k + 1], 127.0, ALU.mult, ALU.min))
                    ch(dve.tensor_scalar(wrows[:, k, :], wrows[:, k, :], -127.0, ROUND, ALU.max, ALU.add))
                    ch(dve.tensor_scalar(wq8[:, k, :], wrows[:, k, :], -ROUND, None, ALU.add))
                ch(dve.tensor_copy(winv[:], wamax[:]))
                for k in range(KC):
                    if k == 1:
                        dve.wait_ge(w_ps, 3 * j + 2)
                    ch(dve.tensor_copy(scale_cols[:], winv[:, k:k + 1].to_broadcast([P, P])))
                dve.wait_ge(w_ps, 3 * j + 3)
                wT = pTb.rearrange("p (o i r) -> p i o r", o=KC, i=KC)
                dve.tensor_copy(qwT[n][:].rearrange("p i (o r) -> p i o r", o=KC), wT).then_inc(w_read, 1)
                dve.tensor_scalar(sw[n][:], pQK[:, 0:C], {"q": 0.25, "o": 1.0}[n], None, ALU.mult).then_inc(w_read, 1)
                dve.tensor_scalar(bias[n][:], W[f"L3_b{n}"][:, 0, :], {"q": 0.25, "o": 1.0}[n], None, ALU.mult)

            def front(b, p):
                nm.front(dve, b, p)
                qx.vector(dve, b, nm.xn[p][:], nm.xn_ready)
                dve.wait_ge(qkv_ps, b + 1)
                dve.tensor_scalar(qpre[:], pQK[:, 0:C], qx.step[:, 0:1], None, ALU.mult).then_inc(q_steps, 1)
                dve.wait_ge(q_steps, 2 * b + 1)
                dve.tensor_tensor(qpre[:], qpre[:], sw["q"][:], ALU.mult).then_inc(q_steps, 1)
                dve.wait_ge(q_steps, 2 * b + 2)
                after(dve, tq.turned_ps, b)
                dve.tensor_tensor(tq.q[:, :, 0:HD], heads(qpre[:]), heads(bias["q"][:]), ALU.add)
                dve.tensor_tensor(tq.k[:, :, 0:HD], heads(pQK[:, C:2 * C]), heads(W["L3_bk"][:, 0, :]),
                                  ALU.add).then_inc(tq.rows_ready, 1)
                if not (isinstance(b, int) and b < 2):
                    dve.wait_ge(sm.pv_done, 4 * (b - 1))
                dve.tensor_tensor(v[p][:], pV[:, 0:C], W["L3_bv"][:, 0, :], ALU.add).then_inc(kv_read, 1)

            def body(b, p):
                sm.vector(dve, b, p)
                sm.normalise(dve, att[:], b, att_ready)
                dve.wait_ge(att_ready, b + 1)
                qa.vector(dve, b, att[:], att_ready)
                dve.wait_ge(out_ps, b + 1)
                dve.tensor_scalar(outp[:], pT[:, C:2 * C], qa.step[:, 0:1], None, ALU.mult).then_inc(out_steps, 1)
                dve.wait_ge(out_steps, 3 * b + 1)
                dve.tensor_tensor(outp[:], outp[:], sw["o"][:], ALU.mult).then_inc(out_steps, 1)
                dve.wait_ge(out_steps, 3 * b + 2)
                dve.tensor_tensor(outp[:], outp[:], bias["o"][:], ALU.add).then_inc(out_steps, 1)
                dve.wait_ge(out_steps, 3 * b + 3)
                x = G["x_all"][:, b, :]
                dve.scalar_tensor_tensor(x, outp[:], G["tg"][:, 3:4], x, ALU.mult, ALU.add).then_inc(added, 1)

            sweep(dve, front, body)


class Quant:

    def __init__(self, ph, G, name, n, floor, peak_floor=None):
        self.G, self.floor, self.peak_floor = G, floor, peak_floor
        self.steps, self.ready = ph.sem(f"{name}_steps"), ph.sem(f"{name}_ready")
        self.peak, self.step, self.inv = (ph.sb(f"{name}_{m}", [P, 1]) for m in ("peak", "step", "inv"))
        self.y = ph.sb(f"{name}_y", [P, n])
        self.q = ph.sb(f"{name}_q", [P, n], BF16)

    def vector(self, dve, b, x, x_ready, x_count=1):
        st = 4 * b
        dve.wait_ge(x_ready, x_count * (b + 1))
        dve.tensor_reduce(self.peak[:], x, AX.X, ALU.max, apply_absolute_value=True).then_inc(self.steps, 1)
        dve.wait_ge(self.steps, st + 1)
        if self.peak_floor is None:
            dve.tensor_scalar(self.step[:], self.peak[:], 1.0 / 127.0, self.floor, ALU.mult, ALU.max).then_inc(self.steps, 1)
        else:
            dve.tensor_scalar(self.step[:], self.peak[:], self.peak_floor, 1.0 / 127.0, ALU.max, ALU.mult
                              ).then_inc(self.steps, 1)
        dve.wait_ge(self.steps, st + 2)
        dve.reciprocal(self.inv[:], self.step[:]).then_inc(self.steps, 1)
        dve.wait_ge(self.steps, st + 3)
        dve.tensor_scalar(self.y[:], x, self.inv[:, 0:1], ROUND, ALU.mult, ALU.add).then_inc(self.steps, 1)
        dve.wait_ge(self.steps, st + 4)
        dve.tensor_scalar(self.q[:], self.y[:], -ROUND, None, ALU.add).then_inc(self.ready, 1)



def phase_l2_attention(nc, D, G):
    W, x_all = G["W"], G["x_all"]
    D4 = 4 * P
    with Phase(nc, "l2x") as ph:
        pT, pQ, pTq, pOT = (ph.ps(n) for n in ("pT", "pQ", "pTq", "pOT"))
        pS, pP = [ph.ps("pS0"), ph.ps("pS1")], [ph.ps("pP0"), ph.ps("pP1")]
        nm = Norm(ph, G, pT)
        cT = [ph.sb(f"cT{i}", [P, KC, P]) for i in range(2)]
        kT = [ph.sb(f"kT{i}", [P, 4, 2, P]) for i in range(2)]
        v = [ph.sb(f"v{i}", [P, 2, D4]) for i in range(2)]
        qT = [ph.sb(f"qT{i}", [P, 4, P]) for i in range(2)]
        cos_q, sin_q, cos_k, sin_k = (ph.sb(n, [P, P]) for n in ("cos_q", "sin_q", "cos_k", "sin_k"))
        cos, sin, wrow = ph.sb("cos", [P, P]), ph.sb("sin", [P, P]), ph.sb("wrow", [P, 2, P])
        mask = ph.sb("mask", [P, 2, 2, P], BF16)
        square = [ph.sb(f"square{i}", [P, 4, P]) for i in range(2)]
        ssq = [ph.sb(f"ssq{i}", [P, 4]) for i in range(2)]
        rms_q = [ph.sb(f"rms_q{i}", [P, 4]) for i in range(4)]
        rms_k = [ph.sb(f"rms_k{i}", [P, 4]) for i in range(2)]
        part = [[ph.sb(f"part{i}{j}", [P, 4, P]) for j in range(2)] for i in range(2)]
        rows = [ph.sb(f"rows{i}", [P, 4, P]) for i in range(2)]
        krows = ph.sb("krows", [P, 4, P])
        prob = ph.sb("prob", [P, 4, 2 * P])
        probT = ph.sb("probT", [P, 2, 4, P])
        oT = ph.sb("oT", [P, 4, P])
        negmax, nb, sums, rec = (ph.sb(n, [P, 4]) for n in ("negmax", "nb", "sums", "rec"))
        eps128 = ph.sb("eps128", [P, 4])
        names = ("const_in", "tables", "cT_ready", "proj_ps", "sq_done", "mul_done", "rms_steps", "add_done",
                 "krows_ready", "turned", "turn_read", "v_ps", "v_read", "sc_ps", "max_steps", "nb_ready", "exp_done",
                 "rec_ready", "prob_ready", "pT_ps", "pT_read_a", "pT_read_v", "ot_ps", "ot_read", "out_ps", "added")
        S = {n: ph.sem(n) for n in names}
        spare = G["spare"]
        block = ph.block()

        def run(eng, prepare0, slot, finish):
            prepare0()
            for g in range(4):
                slot(0, 0, g, False)
            with eng.Fori(0, B // 2 - 1) as i:
                for g in range(4):
                    slot(2 * i + 1, 1, g, False)
                for g in range(4):
                    slot(2 * i + 2, 0, g, False)
            for g in range(4):
                slot(B - 1, 1, g, True)
            finish()

        @block.sync
        def _(sp):
            for dst, src in ((cos[:], D["c_cos"]), (sin[:], D["c_sin"]), (mask[:].bitcast(U16), D["c_mask2"]),
                             (wrow[:, 0, :], D["L2_q_norm"].partition_broadcast(P)),
                             (wrow[:, 1, :], D["L2_k_norm"].partition_broadcast(P)),
                             (eps128[:], D["c_eps128"])):
                sp.dma_start(dst, src).then_inc(S["const_in"], 16)

        def unit_w(u):
            if u == 0:
                return W["l2_wk"], slice(None)
            if u == 1:
                return W["l2_wkc"], slice(None)
            return W["l2_wq"], slice((u - 2) * D4, (u - 1) * D4)

        @block.tensor
        def _(pe):
            pe.wait_ge(*G["loaded"]["l2"])
            pe.wait_ge(S["const_in"], 96)

            def proj(b, p, u):
                U = 6 * b + u
                after(pe, S["sq_done"], U)
                after(pe, S["mul_done"], U)
                if u == 0:
                    pe.wait_ge(nm.xT_ready, b + 1)
                    pe.wait_ge(cT_sem, b + 1)
                w, cols = unit_w(u)
                project(pe, pQ[:], cT[p] if u == 1 else nm.xT[p], w, cols).then_inc(S["proj_ps"], 1)

            cT_sem = S["cT_ready"]

            def trans(b, p, u):
                U = 6 * b + u
                if u < 2:
                    pe.wait_ge(S["krows_ready"], 2 * b + u + 1)
                    src = krows
                else:
                    pe.wait_ge(S["add_done"], 5 * b + u)
                    src = rows[u % 2]
                after(pe, S["turn_read"], U)
                for h in range(4):
                    last = pe.transpose(pTq[:, h * P:(h + 1) * P], src[:, h, :], G["ident"][:])
                last.then_inc(S["turned"], 1)

            def value_rows(b, p, which):
                n = 2 * b + (1 - which)
                after(pe, S["v_read"], n)
                project(pe, pOT[:], (cT if which == 0 else nm.xT)[p], W["l2_wvc"] if which == 0 else W["l2_wv"]
                        ).then_inc(S["v_ps"], 1)

            def scores(b, p, g):
                N = 4 * b + g
                pe.wait_ge(S["turn_read"], 6 * b + g + 3)
                for j in range(2):
                    pe.matmul(pS[j][:], lhsT=G["identb"][:], rhs=mask[:].rearrange("p a b c -> p (a b c)"),
                              start=True, stop=True)
                    for h in range(2):
                        last = pe.matmul(pS[j][:, h * 2 * P:(h + 1) * 2 * P], lhsT=qT[g % 2][:, 2 * j + h, :],
                                         rhs=kT[p][:, g, :, :].rearrange("p a k -> p (a k)"), start=False, stop=True,
                                         skip_group_check=True)
                    last.then_inc(S["sc_ps"], 1)

            def values(b, p, g):
                N = 4 * b + g
                pe.wait_ge(S["pT_read_a"], N + 1)
                pe.wait_ge(S["pT_read_v"], N + 1)
                final = isinstance(b, int) and b == B - 1
                pe.wait_ge(S["v_read"], 2 * b + (2 if g < 2 or final else g + 1))
                for a in range(2):
                    last = pe.matmul(pOT[:], lhsT=v[p][:, a, g * P:(g + 1) * P],
                                     rhs=probT[:, a, :, :].rearrange("p h t -> p (h t)"), start=(a == 0),
                                     stop=(a == 1))
                last.then_inc(S["ot_ps"], 1)

            def output(b, g):
                pe.wait_ge(S["ot_read"], 4 * b + g + 1)
                for h in range(4):
                    last = pe.matmul(pT[:, C:2 * C], lhsT=oT[:, h, :], rhs=W["l2_wo"][:, 4 * g + h, :],
                                     start=(h == 0), stop=(h == 3))
                last.then_inc(S["out_ps"], 1)

            def turn_probs(b, g):
                for j in range(2):
                    pe.wait_ge(S["prob_ready"], 2 * (4 * b + g) + j + 1)
                    for h in range(2):
                        for a in range(2):
                            last = pe.transpose(pP[j][:, (2 * h + a) * P:(2 * h + a + 1) * P],
                                                prob[:, 2 * j + h, a * P:(a + 1) * P], G["ident"][:])
                    last.then_inc(S["pT_ps"], 1)

            def prepare0():
                nm.tensor(pe, 0, 0)
                proj(0, 0, 0)
                value_rows(0, 0, 1)
                trans(0, 0, 0)
                proj(0, 0, 1)
                value_rows(0, 0, 0)
                trans(0, 0, 1)
                proj(0, 0, 2)
                trans(0, 0, 2)
                proj(0, 0, 3)

            def slot(b, p, g, last):
                first = isinstance(b, int) and b == 0 and g == 0
                scores(b, p, g)
                if not first:
                    values(b if g else b - 1, p if g else 1 - p, (g - 1) % 4)
                if g < 2:
                    proj(b, p, g + 4)
                elif not last:
                    if g == 2:
                        proj(b + 1, 1 - p, 0)
                    else:
                        proj(b + 1, 1 - p, 2)
                if not first:
                    output(b if g else b - 1, (g - 1) % 4)
                if g < 3:
                    trans(b, p, g + 3)
                elif not last:
                    trans(b + 1, 1 - p, 1)
                turn_probs(b, g)
                if not last:
                    if g == 0:
                        nm.tensor(pe, b + 1, 1 - p)
                    if g == 2:
                        value_rows(b + 1, 1 - p, 1)
                        trans(b + 1, 1 - p, 0)
                        proj(b + 1, 1 - p, 1)
                    if g == 3:
                        value_rows(b + 1, 1 - p, 0)
                        trans(b + 1, 1 - p, 2)
                        proj(b + 1, 1 - p, 3)

            def finish():
                values(B - 1, 1, 3)
                output(B - 1, 3)

            run(pe, prepare0, slot, finish)

        @block.scalar
        def _(act):
            def squares(b, p, u):
                act.wait_ge(S["proj_ps"], 6 * b + u + 1)
                for h in range(4):
                    ins = act.activation(square[u % 2][:, h, :], pQ[:, h * P:(h + 1) * P], ACT.Square,
                                         accum_out=ssq[u % 2][:, h:h + 1])
                ins.then_inc(S["sq_done"], 1)

            def evacuate(b, p, u):
                act.wait_ge(S["turned"], 6 * b + u + 1)
                t = pTq[:].rearrange("p (h k) -> p h k", h=4)
                dst = qT[u % 2][:] if u >= 2 else kT[p][:, :, 1 - u, :]
                act.activation(dst, t, ACT.Copy).then_inc(S["turn_read"], 1)

            def value_rows(b, p, which):
                act.wait_ge(S["v_ps"], 2 * b + (1 - which) + 1)
                act.activation(v[p][:, which, :], pOT[:], ACT.Copy).then_inc(S["v_read"], 1)

            def exps(b, g):
                N = 4 * b + g
                for j in range(2):
                    act.wait_ge(S["nb_ready"], 2 * N + j + 1)
                    for h in (2 * j, 2 * j + 1):
                        ins = act.activation(prob[:, h, :], pS[j][:, (h % 2) * 2 * P:(h % 2 + 1) * 2 * P], ACT.Exp,
                                             scale=rms_q[g][:, h:h + 1], bias=nb[:, h:h + 1],
                                             accum_out=sums[:, h:h + 1])
                    ins.then_inc(S["exp_done"], 1)

            def values(b, g):
                act.wait_ge(S["ot_ps"], 4 * b + g + 1)
                act.activation(oT[:].rearrange("p h t -> p (h t)"), pOT[:], ACT.Copy).then_inc(S["ot_read"], 1)

            def probs(b, g):
                act.wait_ge(S["pT_ps"], 2 * (4 * b + g) + 1)
                act.activation(probT[:, :, 0:2, :], pP[0][:].rearrange("p (h a t) -> p a h t", h=2, a=2),
                               ACT.Copy).then_inc(S["pT_read_a"], 1)

            def prepare0():
                nm.scalar(act, 0, 0)
                squares(0, 0, 0)
                value_rows(0, 0, 1)
                evacuate(0, 0, 0)
                squares(0, 0, 1)
                value_rows(0, 0, 0)
                evacuate(0, 0, 1)
                squares(0, 0, 2)
                evacuate(0, 0, 2)
                squares(0, 0, 3)

            def slot(b, p, g, last):
                first = isinstance(b, int) and b == 0 and g == 0
                exps(b, g)
                if not first:
                    values(b if g else b - 1, (g - 1) % 4)
                if g < 2:
                    squares(b, p, g + 4)
                elif not last:
                    squares(b + 1, 1 - p, 0 if g == 2 else 2)
                if g < 3:
                    evacuate(b, p, g + 3)
                elif not last:
                    evacuate(b + 1, 1 - p, 1)
                probs(b, g)
                if not last:
                    if g == 0:
                        nm.scalar(act, b + 1, 1 - p)
                    if g >= 2:
                        value_rows(b + 1, 1 - p, 3 - g)
                        evacuate(b + 1, 1 - p, 0 if g == 2 else 2)
                        squares(b + 1, 1 - p, 1 if g == 2 else 3)

            run(act, prepare0, slot, lambda: values(B - 1, 3))

        @block.gpsimd
        def _(pool):
            def unit(b, p, u):
                U = 6 * b + u
                r = rms_k[u] if u < 2 else rms_q[u - 2]
                pool.wait_ge(S["sq_done"], U + 1)
                pool.tensor_tensor(r[:], ssq[u % 2][:], eps128[:], ALU.add).then_inc(S["rms_steps"], 1)
                pool.wait_ge(S["rms_steps"], 2 * U + 1)
                pool.tensor_tensor(r[:], r[:], G["minus_half"][:, 0:4], ALU.pow).then_inc(S["rms_steps"], 1)
                if u != 1:
                    pool.wait_ge(S["mul_done"], U + 1)
                    pool.tensor_tensor(rows[u % 2][:], part[u % 2][0][:], part[u % 2][1][:],
                                       ALU.add).then_inc(S["add_done"], 1)

            def ctx(b, p):
                pool.tensor_copy(cT[p][:], G["ctxT"][:, :, bass.ds(b * P, P)]).then_inc(S["cT_ready"], 1)

            def prepare0():
                ctx(0, 0)
                nm.pool(pool, 0, 0)
                for u in range(4):
                    unit(0, 0, u)

            def slot(b, p, g, last):
                if g == 0 and not last:
                    nm.pool(pool, b + 1, 1 - p)
                if g < 2:
                    unit(b, p, g + 4)
                elif not last:
                    unit(b + 1, 1 - p, 0 if g == 2 else 2)
                if g == 1 and not last:
                    ctx(b + 1, 1 - p)
                if g >= 2 and not last:
                    unit(b + 1, 1 - p, 1 if g == 2 else 3)

            run(pool, prepare0, slot, lambda: None)

        @block.vector
        def _(dve):
            dve.wait_ge(S["const_in"], 96)
            H = P // 2
            for j, (c, s) in enumerate(((cos_q, sin_q), (cos_k, sin_k))):
                dve.tensor_tensor(c[:], cos[:], wrow[:, j, :], ALU.mult)
                dve.tensor_tensor(s[:, 0:H], sin[:, 0:H], wrow[:, j, H:P], ALU.mult)
                dve.tensor_tensor(s[:, H:P], sin[:, H:P], wrow[:, j, 0:H], ALU.mult).then_inc(S["tables"], 1)
            dve.wait_ge(S["tables"], 2)

            def wide(t):
                return t.unsqueeze(1).to_broadcast([P, 4, t.shape[1]])

            def mul(b, p, u):
                U = 6 * b + u
                q = pQ[:].rearrange("p (h d) -> p h d", h=4)
                dve.wait_ge(S["sq_done"], U + 1)
                if u == 1:
                    dve.tensor_tensor(part[1][0][:], q, wide(wrow[:, 1, :]), ALU.mult).then_inc(S["mul_done"], 1)
                    return
                c, s = (cos_k, sin_k) if u == 0 else (cos_q, sin_q)
                a, r = part[u % 2]
                dve.tensor_tensor(a[:], q, wide(c[:]), ALU.mult)
                dve.tensor_tensor(r[:, :, 0:H], q[:, :, H:P], wide(s[:, 0:H]), ALU.mult)
                dve.tensor_tensor(r[:, :, H:P], q[:, :, 0:H], wide(s[:, H:P]), ALU.mult).then_inc(S["mul_done"], 1)

            def key_norm(b, p, u):
                if u == 0:
                    dve.wait_ge(S["add_done"], 5 * b + 1)
                    src = rows[0]
                else:
                    dve.wait_ge(S["rms_steps"], 2 * (6 * b + u) + 2)
                    dve.wait_ge(S["mul_done"], 6 * b + u + 1)
                    src = part[1][0]
                after(dve, S["turned"], 6 * b + (u if u else -4))
                dve.scalar_tensor_tensor(krows[:], src[:], float(np.sqrt(P)), bc(rms_k[u][:], P), ALU.mult,
                                         ALU.mult).then_inc(S["krows_ready"], 1)

            def maxima(b, g):
                N = 4 * b + g
                for j in range(2):
                    c = slice(2 * j, 2 * j + 2)
                    dve.wait_ge(S["sc_ps"], 2 * N + j + 1)
                    dve.tensor_reduce(negmax[:, c], pS[j][:].rearrange("p (h k) -> p h k", h=2), AX.X, ALU.max,
                                      negate=True).then_inc(S["max_steps"], 1)
                    dve.wait_ge(S["max_steps"], 2 * N + j + 1)
                    dve.tensor_tensor(nb[:, c], negmax[:, c], rms_q[g][:, c], ALU.mult).then_inc(S["nb_ready"], 1)

            def divide(b, g):
                N = 4 * b + g
                for j in range(2):
                    c = slice(2 * j, 2 * j + 2)
                    dve.wait_ge(S["exp_done"], 2 * N + j + 1)
                    dve.reciprocal(rec[:, c], sums[:, c]).then_inc(S["rec_ready"], 1)
                    dve.wait_ge(S["rec_ready"], 2 * N + j + 1)
                    for h in (2 * j, 2 * j + 1):
                        ins = dve.tensor_scalar(prob[:, h, :], prob[:, h, :], rec[:, h:h + 1], None, ALU.mult)
                    ins.then_inc(S["prob_ready"], 1)

            def add_out(b, g):
                dve.wait_ge(S["out_ps"], 4 * b + g + 1)
                after(dve, S["added"], 4 * b + g)
                x = x_all[:, b, :]
                dve.scalar_tensor_tensor(x, pT[:, C:2 * C], G["tg"][:, 2:3], x, ALU.mult,
                                         ALU.add).then_inc(S["added"], 1)

            def probs(b, g):
                dve.wait_ge(S["pT_ps"], 2 * (4 * b + g) + 2)
                dve.tensor_copy(probT[:, :, 2:4, :], pP[1][:].rearrange("p (h a t) -> p a h t", h=2, a=2)
                                ).then_inc(S["pT_read_v"], 1)

            def prepare0():
                nm.front(dve, 0, 0)
                mul(0, 0, 0)
                key_norm(0, 0, 0)
                mul(0, 0, 1)
                key_norm(0, 0, 1)
                mul(0, 0, 2)
                mul(0, 0, 3)

            def slot(b, p, g, last):
                first = isinstance(b, int) and b == 0 and g == 0
                maxima(b, g)
                if g == 0 and not last:
                    nm.vector(dve, b + 1, 1 - p)
                if g < 2:
                    mul(b, p, g + 4)
                elif not last:
                    mul(b + 1, 1 - p, 0 if g == 2 else 2)
                if not first:
                    add_out(b if g else b - 1, (g - 1) % 4)
                divide(b, g)
                if g == 0 and not last:
                    nm.normalise(dve, b + 1, 1 - p)
                if g == 2 and not last:
                    key_norm(b + 1, 1 - p, 0)
                probs(b, g)
                if g >= 2 and not last:
                    mul(b + 1, 1 - p, 1 if g == 2 else 3)
                if g == 2 and not last:
                    key_norm(b + 1, 1 - p, 1)

            run(dve, prepare0, slot, lambda: add_out(B - 1, 3))


def phase_l2_ffn(nc, D, G):
    W = G["W"]
    HID = 1024
    HT = HID // P
    with Phase(nc, "l2f") as ph:
        pT = ph.ps("pT")
        pG = [ph.ps(f"pG{i}") for i in range(2)]
        pV = [ph.ps(f"pV{i}") for i in range(2)]
        pH = ph.ps("pH", BF16)
        pTb = pT[:, 0:P].bitcast(BF16)
        nm = Norm(ph, G, None)
        qx, qh = Quant(ph, G, "qx", C, None, 1e-5), Quant(ph, G, "qh", HID, None, 1e-5)
        wq = {n: ph.sb(f"{n}_q", list(W[n].shape), BF16) for n in ("l2f_gate", "l2f_val", "l2f_out")}
        gam = ph.sb("gam", [P, 3])
        ginv = ph.sb("ginv", [P, 3])
        wsum = ph.sb("wsum", [P, 3])
        ones = ph.sb("ones", [P, P])
        wtmp = ph.sb("wtmp", [P, 2048])
        rows = {n: ph.sb(f"{n}_row", [P, k]) for n, k in (("gate_b", HID), ("val_b", HID), ("out_b", C))}
        xqT = [ph.sb(f"xqT{i}", [P, KC, P], BF16) for i in range(2)]
        hqT = ph.sb("hqT", [P, HT, P], BF16)
        scale = ph.sb("scale", [P, 3])
        gate, val, hid = ph.sb("gate", [P, HID]), ph.sb("val", [P, HID]), ph.sb("hid", [P, HID])
        (const_in, wsteps, wsum_ps, xq_ps, xqT_ready, gv_ps, scaled, gate_ready, silu_done, val_ready, hid_done,
         hq_ps, hqT_ready, out_ps, out_scale, added) = (
            ph.sem(n) for n in ("const_in", "wsteps", "wsum_ps", "xq_ps", "xqT_ready", "gv_ps", "scaled",
                                "gate_ready", "silu_done", "val_ready", "hid_done", "hq_ps", "hqT_ready", "out_ps",
                                "out_scale", "added"))
        block = ph.block()

        @block.sync
        def _(sp):
            for n in ("gate_b", "val_b", "out_b"):
                sp.dma_start(rows[n][:], D[f"L2_{n}"].partition_broadcast(P)).then_inc(const_in, 16)
            G["load"](sp, "l3f")

        @block.gpsimd
        def _(pool):
            sweep(pool, lambda b, p: nm.pool(pool, b, p), lambda b, p: None)

        @block.tensor
        def _(pe):
            pe.wait_ge(wsteps, 4)
            pe.matmul(pT[:, 0:3], lhsT=ones[:], rhs=wsum[:], start=True, stop=True).then_inc(wsum_ps, 1)

            def front(b, p):
                pe.wait_ge(qx.ready, b + 1)
                after(pe, xqT_ready, b)
                for k in range(KC):
                    last = pe.transpose(pTb[:, k * P:(k + 1) * P], qx.q[:, k * P:(k + 1) * P], G["identb"][:])
                last.then_inc(xq_ps, 1)

            def body(b, p):
                pe.wait_ge(xqT_ready, b + 1)
                for j in range(2):
                    after(pe, val_ready, 2 * b + j - 1)
                    project(pe, pG[j][:], xqT[p], wq["l2f_gate"], slice(j * 512, j * 512 + 512))
                    project(pe, pV[j][:], xqT[p], wq["l2f_val"], slice(j * 512, j * 512 + 512)).then_inc(gv_ps, 1)
                pe.wait_ge(qh.ready, b + 1)
                for t in range(HT):
                    last = pe.transpose(pH[:, t * P:(t + 1) * P], qh.q[:, t * P:(t + 1) * P], G["identb"][:])
                last.then_inc(hq_ps, 1)
                pe.wait_ge(hqT_ready, b + 1)
                for t in range(HT):
                    last = pe.matmul(pT[:, C:2 * C], lhsT=hqT[:, t, :], rhs=wq["l2f_out"][:, t, :], start=(t == 0),
                                     stop=(t == HT - 1))
                last.then_inc(out_ps, 1)

            sweep(pe, front, body)

        @block.scalar
        def _(act):
            def front(b, p):
                act.wait_ge(xq_ps, b + 1)
                act.activation(xqT[p][:].rearrange("p k t -> p (k t)"), pTb, ACT.Copy).then_inc(xqT_ready, 1)

            def body(b, p):
                for j in range(2):
                    c = slice(j * 512, j * 512 + 512)
                    act.wait_ge(gate_ready, 2 * b + j + 1)
                    act.activation(gate[:, c], gate[:, c], ACT.Silu).then_inc(silu_done, 1)
                act.wait_ge(hq_ps, b + 1)
                act.activation(hqT[:].rearrange("p k t -> p (k t)"), pH[:], ACT.Copy).then_inc(hqT_ready, 1)

            sweep(act, front, body)

        @block.vector
        def _(dve):
            dve.wait_ge(*G["loaded"]["l2f"])
            dve.wait_ge(const_in, 48)
            names = ("l2f_gate", "l2f_val", "l2f_out")
            ch = Chain(dve, wsteps, 4 + 3 + 9)
            ch.turn(0)
            ch(dve.memset(ones[:], 1.0))
            for j, n in enumerate(names):
                ch(dve.tensor_reduce(wsum[:, j:j + 1], W[n].rearrange("p a b -> p (a b)"), AX.X, ALU.add,
                                     apply_absolute_value=True))
            dve.wait_ge(wsum_ps, 1)
            ch(dve.tensor_scalar(gam[:], pT[:, 0:3], 1.0 / (HID * C), 1e-5, ALU.mult, ALU.max))
            ch(dve.reciprocal(ginv[:], gam[:]))
            for j, n in enumerate(names):
                w = W[n].rearrange("p a b -> p (a b)")
                ch(dve.tensor_scalar(wtmp[:], w, ginv[:, j:j + 1], 1.0, ALU.mult, ALU.min))
                ch(dve.tensor_scalar(wtmp[:], wtmp[:], -1.0, ROUND, ALU.max, ALU.add))
                ch(dve.tensor_scalar(wq[n][:].rearrange("p a b -> p (a b)"), wtmp[:], -ROUND, None, ALU.add))
            ch(dve.tensor_scalar(rows["out_b"][:], rows["out_b"][:], G["tg"][:, 6:7], None, ALU.mult))

            step = [ph.sb(f"step{i}", [P, 2]) for i in range(2)]

            def front(b, p):
                nm.front(dve, b, p)
                after(dve, xq_ps, b)
                qx.vector(dve, b, nm.xn[p][:], nm.xn_ready)
                dve.tensor_tensor(step[p][:], qx.step[:].to_broadcast([P, 2]), gam[:, 0:2],
                                  ALU.mult).then_inc(scaled, 1)
                dve.wait_ge(scaled, b + 1)

            def body(b, p):
                x = G["x_all"][:, b, :]
                for j in range(2):
                    c = slice(j * 512, j * 512 + 512)
                    dve.wait_ge(gv_ps, 2 * b + j + 1)
                    dve.scalar_tensor_tensor(gate[:, c], pG[j][:], step[p][:, 0:1], rows["gate_b"][:, c], ALU.mult,
                                             ALU.add).then_inc(gate_ready, 1)
                    dve.scalar_tensor_tensor(val[:, c], pV[j][:], step[p][:, 1:2], rows["val_b"][:, c], ALU.mult,
                                             ALU.add).then_inc(val_ready, 1)
                for j in range(2):
                    c = slice(j * 512, j * 512 + 512)
                    dve.wait_ge(silu_done, 2 * b + j + 1)
                    dve.wait_ge(val_ready, 2 * b + j + 1)
                    dve.tensor_tensor(hid[:, c], gate[:, c], val[:, c], ALU.mult).then_inc(hid_done, 1)
                qh.vector(dve, b, hid[:], hid_done, 2)
                dve.tensor_scalar(scale[:, 0:1], qh.step[:], gam[:, 2:3], G["tg"][:, 6:7], ALU.mult,
                                  ALU.mult).then_inc(out_scale, 1)
                dve.wait_ge(out_scale, 2 * b + 1)
                dve.tensor_tensor(x, x, rows["out_b"][:], ALU.add).then_inc(out_scale, 1)
                dve.wait_ge(out_scale, 2 * b + 2)
                dve.wait_ge(out_ps, b + 1)
                dve.scalar_tensor_tensor(x, pT[:, C:2 * C], scale[:, 0:1], x, ALU.mult, ALU.add).then_inc(added, 1)

            sweep(dve, front, body)


def phase_gating3(nc, D, G):
    NE = 8
    with Phase(nc, "gate3") as ph:
        pT, pL = ph.ps("pT"), ph.ps("pL")
        nm = Norm(ph, G, pT)
        bias = ph.sb("bias", [P, NE])
        score, pick = ph.sb("score", [P, B, NE]), ph.sb("pick", [P, B, NE])
        top, replaced = ph.sb("top", [P, B, 8]), ph.sb("replaced", [P, B, NE])
        red, rec = ph.sb("red", [P, B]), ph.sb("rec", [P, B])
        const_in, logits, steps, exp_done = (ph.sem(n) for n in ("const_in", "logits", "steps", "exp_done"))
        block = ph.block()
        FLOOR = -3.0e38

        @block.gpsimd
        def _(pool):
            sweep(pool, lambda b, p: nm.pool(pool, b, p), lambda b, p: None)

        @block.sync
        def _(sp):
            sp.dma_start(bias[:], D["L3_expert_bias"].partition_broadcast(P)).then_inc(const_in, 16)

        @block.tensor
        def _(pe):
            def body(b, p):
                pe.wait_ge(nm.xT_ready, b + 1)
                project(pe, pL[:, bass.ds(b * NE, NE)], nm.xT[p], G["W"]["L3_router"]).then_inc(logits, 1)

            sweep(pe, lambda b, p: nm.tensor(pe, b, p), body)

        @block.scalar
        def _(act):
            def front(b, p):
                act.wait_ge(nm.xT_ps, b + 1)
                act.activation(G["xnT"][:, :, bass.ds(b * P, P)], pT[:, 0:C].rearrange("p (k t) -> p k t", k=KC),
                               ACT.Copy)
                nm.scalar(act, b, p)

            front(0, 0)
            front(1, 1)
            with act.Fori(1, B // 2) as i:
                act.wait_ge(logits, 2 * i - 1)
                front(2 * i, 0)
                act.wait_ge(logits, 2 * i)
                front(2 * i + 1, 1)
            act.wait_ge(logits, B)
            act.activation(score[:].rearrange("p b e -> p (b e)"), pL[:, 0:B * NE], ACT.Exp,
                           scale=-1.0).then_inc(exp_done, 1)

        @block.vector
        def _(dve):
            sweep(dve, lambda b, p: nm.front(dve, b, p), lambda b, p: None)
            ch = Chain(dve, steps, 3 + 1 + 2 * B + 5)
            ch.turn(0)
            dve.wait_ge(exp_done, 1)
            dve.wait_ge(const_in, 16)
            ch(dve.tensor_scalar(score[:], score[:], 1.0, None, ALU.add))
            ch(dve.reciprocal(score[:], score[:]))
            ch(dve.tensor_tensor(pick[:], score[:], bias[:].unsqueeze(1).to_broadcast([P, B, NE]), ALU.add))
            for b in range(B):
                ch(dve.max(top[:, b, :], pick[:, b, :]))
            ch(dve.memset(top[:, :, 2:8], FLOOR))
            for b in range(B):
                ch(dve.match_replace(replaced[:, b, :], top[:, b, :], pick[:, b, :], -FLOOR))
            ch(dve.tensor_scalar(pick[:], replaced[:], -FLOOR, None, ALU.is_equal))
            ch(dve.tensor_tensor(score[:], score[:], pick[:], ALU.mult))
            ch(dve.tensor_reduce(red[:], score[:], AX.X, ALU.add))
            ch(dve.tensor_scalar(red[:], red[:], 1e-9, None, ALU.add))
            ch(dve.reciprocal(rec[:], red[:]))
            dve.tensor_tensor(G["w_all"][:], score[:], bc(rec[:], NE), ALU.mult)



def program(nc, D, out):
    with ExitStack() as top:
        def sb(name, shape, dt=F32):
            return top.enter_context(nc.sbuf_tensor(name, shape, dt))

        G = {}
        G["x_all"] = sb("x_all", [P, B, C])
        G["ctxT"] = sb("ctxT", [P, KC, B * P])
        G["ident"], G["identb"] = sb("ident", [P, P]), sb("identb", [P, P], BF16)
        G["tg"] = sb("tg", [P, 8])
        G["minus_half"], G["eps"] = sb("minus_half", [P, 16]), sb("eps", [P, 1])
        G["spare"] = top.enter_context(nc.semaphore("spare"))
        big = sb("big", [P, 18432])
        small = sb("small", [P, SMALL_COLS])
        sems = {k: top.enter_context(nc.semaphore(f"in_{k}")) for k in ("moe", "small", "l2", "l3f", "l2f")}
        G["loaded"] = {"moe": (sems["moe"], 48), "small": (sems["small"], 16 * len(SMALL)),
                       "l2": (sems["l2"], 16 * 6), "l2f": (sems["l2f"], 48), "l3f": (sems["l3f"], 48)}

        def cut(t, at, k, n):
            return t[:, at:at + k * n].rearrange("p (k n) -> p k n", k=k)

        W = {}
        W["e_gate"], W["e_up"], W["e_down"] = cut(big, 0, 2, 3072), cut(big, 6144, 2, 3072), cut(big, 12288, 24, C)
        at = 0
        for name, k, n in BIG_L2:
            W[name] = cut(big, at, k, n)
            at += k * n
        at = 0
        for name, k, n in BIG_L3:
            W[name] = cut(big, at, k, n)
            at += k * n
        at = 0
        for name, k, n in SMALL:
            W[name] = cut(small, at, k, n)
            at += k * n
        G["l0_gate_w"] = W["L0_ffn_gate_w"]
        G["W"] = W

        def load(sp, what):
            if what == "moe":
                for n in ("e_gate", "e_up", "e_down"):
                    sp.dma_start(W[n], D[n]).then_inc(sems["moe"], 16)
            if what in ("l2", "l2f", "l3f"):
                for n in {"l2": BIG_L2[:6], "l2f": BIG_L2[6:], "l3f": BIG_L3}[what]:
                    sp.dma_start(W[n[0]], D[n[0]]).then_inc(sems[what], 16)
            if what == "small":
                for name, k, n in SMALL:
                    src = D[name].partition_broadcast(P) if k == 1 else D[name]
                    dst = W[name][:, 0, :] if k == 1 else W[name]
                    sp.dma_start(dst, src).then_inc(sems["small"], 16)
        G["load"] = load

        phase_setup(nc, D, G)
        if UPTO >= 1:
            phase_hyena(nc, D, G)
        if UPTO >= 2:
            with Phase(nc, "moe_data") as md:
                G["xnT"], G["w_all"] = md.sb("xnT", [P, KC, B * P]), md.sb("w_all", [P, B, 32])
                phase_gating0(nc, D, G)
                gated_mlp(nc, G, "moe", 4, lambda k, c: W["e_gate"][:, k, c * 384:(c + 1) * 384],
                          lambda k, c: W["e_up"][:, k, c * 384:(c + 1) * 384],
                          lambda t: W["e_down"][:, t, :], 3072, 384,
                          lambda b, c: G["w_all"][:, b, 4 * c:4 * c + 4], [G["loaded"]["moe"]])

        if UPTO >= 3:
            phase_l1_attention(nc, D, G)
        if UPTO >= 4:
            phase_l1_ffn(nc, D, G)
        if UPTO >= 5:
            phase_l2_attention(nc, D, G)
        if UPTO >= 6:
            phase_l2_ffn(nc, D, G)
        if UPTO >= 7:
            phase_l3_attention(nc, D, G)
        if UPTO >= 8:
            with Phase(nc, "l3_data") as md:
                G["xnT"], G["w_all"] = md.sb("xnT", [P, KC, B * P]), md.sb("w_all", [P, B, 8])
                phase_gating3(nc, D, G)
                gated_mlp(nc, G, "l3f", 7, lambda k, c: W["f_gate"][:, k, c * 512:(c + 1) * 512],
                          lambda k, c: W["f_up"][:, k, c * 512:(c + 1) * 512],
                          lambda t: W["f_down"][:, t, :], 2048, 512,
                          lambda b, c: None if c < 2 else G["w_all"][:, b, 4 * (c - 2):4 * (c - 2) + 4],
                          [G["loaded"]["l3f"]])

        with Phase(nc, "store") as ph:
            stored = ph.sem("stored")
            block = ph.block()

            @block.sync
            def _(sp):
                sp.dma_start(out.rearrange("b t c -> t b c"), G["x_all"][:]).then_inc(stored, 16)
                sp.wait_ge(stored, 16)


BIG_L2 = [("l2_wq", 2, 2048), ("l2_wk", 2, 512), ("l2_wv", 2, 512), ("l2_wkc", 2, 512), ("l2_wvc", 2, 512),
          ("l2_wo", 16, C), ("l2f_gate", 2, 1024), ("l2f_val", 2, 1024), ("l2f_out", 8, C)]
BIG_L3 = [("f_gate", 2, 2048), ("f_up", 2, 2048), ("f_down", 16, C)]
SMALL = [("L0_ffn_gate_w", 2, 32),
         ("L1_xattn_Wq", 2, C), ("L1_xattn_Wk", 2, C), ("L1_xattn_Wv", 2, C), ("L1_xattn_Wo", 2, C),
         ("L1_xattn_bq", 1, C), ("L1_xattn_bk", 1, C), ("L1_xattn_bv", 1, C), ("L1_xattn_bo", 1, C),
         ("L1_xattn_ln_gamma", 1, C), ("L1_xattn_ln_beta", 1, C), ("L1_xattn_residual_scale", 1, 1),
         ("W_qk", 2, 2 * C), ("W_vg", 2, C + NH),
         ("L3_router", 2, 8), ("L3_wq", 2, C), ("L3_wk", 2, C), ("L3_wv", 2, C), ("L3_wo", 2, C),
         ("L3_bq", 1, C), ("L3_bk", 1, C), ("L3_bv", 1, C), ("L3_bo", 1, C)]
SMALL_COLS = sum(k * n for _, k, n in SMALL)


def tiles(w):
    k, n = w.shape
    return np.ascontiguousarray(w.reshape(k // P, P, n).transpose(1, 0, 2))


def bf16_bits(a):
    return (np.ascontiguousarray(a, np.float32).view(np.uint32) >> 16).astype(np.uint16)


def constants():
    t = np.arange(P)
    eye = np.eye(P, dtype=np.float32)
    freq = (1.0 / np.float32(10000.0) ** (np.arange(0, P, 2, dtype=np.float32) / np.float32(P))).astype(np.float32)
    half = np.outer(t.astype(np.float32), freq).astype(np.float32)
    angle = np.concatenate([half, half], axis=1)
    return {
        "c_ident": eye,
        "c_minus_half": np.full((P, 16), -0.5, np.float32),
        "c_eps": np.full((P, 1), LN_EPS, np.float32),
        "c_identb": bf16_bits(eye),
        "c_blockones": (t[:, None] // 8 == t[None, :] // 8).astype(np.float32),
        "c_causal": bf16_bits(np.repeat(np.where(t[None, :] > t[:, None], NEG, 0.0)[:, None, :], 4, axis=1)),
        "c_count": np.arange(NH, dtype=np.float32) - NH,
        "c_mask2": bf16_bits(np.stack([np.zeros((P, P)), np.where(t[None, :] > t[:, None], NEG, 0.0)],
                                      axis=1)[:, None].repeat(2, axis=1)),
        "c_cos": np.cos(angle), "c_sin": np.sin(angle) * np.where(t < 64, -1.0, 1.0).astype(np.float32)[None, :],
        "c_eps128": np.full((P, 4), P * 1e-6, np.float32),
        "c_lower": bf16_bits(t[:, None] < t[None, :]),
        "c_onesb": bf16_bits(np.ones((P, P))),
    }


def lay_out(a):
    d = {n: a[n] for n in ("x", "ctx_2048", "fside_S2_0", "g_xattn", "g_ffn")}
    k = a["L0_xattn_k"]
    d["k_rev"] = np.concatenate([k[:, ::-1], np.zeros((k.shape[0], P - 1), k.dtype)], axis=1)
    d["L0_ffn_gate_w"] = tiles(a["L0_ffn_gate_w"])
    for name, key in (("e_gate", "L0_ffn_w_gate"), ("e_up", "L0_ffn_w_up")):
        d[name] = tiles(a[key].transpose(1, 0, 2).reshape(C, -1))
    for n in ("Wq", "Wk", "Wv", "Wo"):
        d[f"L1_xattn_{n}"] = tiles(a[f"L1_xattn_{n}"].T)
    for n in ("bq", "bk", "bv", "bo", "ln_gamma", "ln_beta"):
        d[f"L1_xattn_{n}"] = a[f"L1_xattn_{n}"]
    d["L1_xattn_residual_scale"] = a["L1_xattn_residual_scale"].reshape(1)
    d["mask_T"] = a["mask_BxS2_ik0"].T
    qkv = a["L1_ffn_W_qkv"]
    d["W_qk"] = tiles(qkv[:2 * C].T)
    d["W_vg"] = tiles(np.concatenate([qkv[2 * C:], a["L1_ffn_W_gate"]], axis=0).T)
    for n in "qo":
        d[f"L3_w{n}"] = tiles(a[f"L3_xattn_w{n}"])
    for n in "kv":
        d[f"L3_w{n}"] = tiles(a[f"L3_xattn_w{n}"].T)
    for n in "qkvo":
        d[f"L3_b{n}"] = a[f"L3_xattn_b{n}"]
    for n in ("wq", "wk", "wv"):
        d[f"l2_{n}"] = tiles(a[f"L2_xattn_{n}"])
    d["l2_wkc"], d["l2_wvc"] = tiles(a["L2_xattn_wk_ctx"]), tiles(a["L2_xattn_wv_ctx"])
    d["l2_wo"] = tiles(a["L2_xattn_wo"])
    d["L2_q_norm"], d["L2_k_norm"] = a["L2_xattn_q_norm_w"], a["L2_xattn_k_norm_w"]
    for n in ("gate", "val", "out"):
        d[f"l2f_{n}"] = tiles(a[f"L2_ffn_{n}_w"].T)
        d[f"L2_{n}_b"] = a[f"L2_ffn_{n}_b"]
    d["L3_router"] = tiles(a["L3_ffn_router_w"].T)
    d["L3_expert_bias"] = a["L3_ffn_expert_bias"]
    w12 = a["L3_ffn_w12"]
    half = w12.shape[1] // 2
    for name, shared, routed in (("f_gate", "L3_ffn_sw1", w12[:, :half]), ("f_up", "L3_ffn_sw2", w12[:, half:])):
        d[name] = tiles(np.concatenate([a[shared], routed.reshape(-1, C)], axis=0).T)
    d["f_down"] = tiles(np.concatenate([a["L3_ffn_sw3"].T, a["L3_ffn_w3"].transpose(0, 2, 1).reshape(-1, C)], axis=0))
    d["mask_BxSxS2_ff0"] = a["mask_BxSxS2_ff0"]
    d["e_down"] = tiles(a["L0_ffn_w_down"].reshape(-1, C))
    return d


def kernel(**inputs):
    import concourse.bacc as bacc
    from concourse.bass_utils import run_bass_kernel_spmd

    nc = bacc.Bacc("TRN2", target_bir_lowering=False, num_devices=1)
    arrays = {n: np.ascontiguousarray(v) for n, v in inputs.items()}
    laid = {**lay_out(arrays), **constants()}
    feed, D = {}, {}
    for n, v in laid.items():
        v = np.ascontiguousarray(v)
        feed[f"in_{n}"] = v
        D[n] = nc.dram_tensor(f"in_{n}", v.shape, mybir.dt.from_np(v.dtype), kind="ExternalInput").ap()
    out = nc.dram_tensor("out_x", (B, P, C), F32, kind="ExternalOutput").ap()
    program(nc, D, out)
    r = run_bass_kernel_spmd(nc, [feed], core_ids=[0])
    return r.results[0]["out_x"]
```
